# Optimizing a Trainium2 kernel written in Bass

```python
import numpy as np
import jax
import jax.numpy as jnp

def _softmax(x, axis=-1):
    return jax.nn.softmax(x, axis=axis)

def _gelu(x):
    return jax.nn.gelu(x, approximate=True)

def _silu(x):
    return jax.nn.silu(x)

def _sigmoid(x):
    return jax.nn.sigmoid(x)

def _layernorm(x, axis=-1, eps=1e-05):
    m = jnp.mean(x, axis=axis, keepdims=True)
    v = jnp.var(x, axis=axis, keepdims=True)
    return (x - m) / jnp.sqrt(v + eps)

def _scatter_add(tgt, idx, src, axis=0):
    return tgt.at[idx].add(src)

def _segment_sum(src, seg, n):
    return jax.ops.segment_sum(src, seg, n)
kernel_name = 'mk_gnn_preln_d2_gnn_r8_8fd543'

def setup_inputs(seed: int=0):
    np.random.seed(seed)
    _w = jnp.asarray

    def _rec_inputs():
        import jax
        import jax.numpy as jnp
        _gk = jax.random.key(seed)
        x = -0.000202 + 1 * jax.random.normal(jax.random.fold_in(_gk, 1), (12500, 64), jnp.float32)
        _s = jax.random.randint(jax.random.fold_in(_gk, 2), (100000,), 0, 12500, jnp.int32)
        _d = jax.random.randint(jax.random.fold_in(_gk, 3), (100000,), 0, 12500, jnp.int32)
        _loop = jnp.arange(12500, dtype=jnp.int32)
        src = jnp.concatenate([_s, _d, _loop])
        dst = jnp.concatenate([_d, _s, _loop])
        _o = jnp.argsort(dst, stable=True)
        src = src[_o]
        dst = dst[_o]
        edge_attr_32 = -9.77346e-05 + 0.999888 * jax.random.normal(jax.random.fold_in(_gk, 12), (212500, 32), jnp.float32)
        edge_type_32 = jax.random.randint(jax.random.fold_in(_gk, 13), (212500,), 0, 32, jnp.int32)
        edge_weight1 = jax.random.uniform(jax.random.fold_in(_gk, 14), (212500, 1), jnp.float32, 0.0, 0.999998)
        return (x, src, dst, edge_attr_32, edge_type_32, edge_weight1)
    x, src, dst, edge_attr_32, edge_type_32, edge_weight1 = _rec_inputs()

    def _L0_gnn_setup():
        import jax, jax.numpy as jnp
        import numpy as np
        N_NODES = 12500
        N_EDGES = 200000
        NODE_F = 64
        EDGE_F = 32
        OUT_F = 64
        HIDDEN = 2 * OUT_F
        IN_F = 2 * NODE_F + EDGE_F
        key = jax.random.key(seed)
        ks = jax.random.split(key, 8)
        nodes = jax.random.normal(ks[0], (N_NODES, NODE_F), dtype=jnp.float32)
        edges = jax.random.normal(ks[1], (N_EDGES, EDGE_F), dtype=jnp.float32)
        senders = jax.random.randint(ks[2], (N_EDGES,), 0, N_NODES, dtype=jnp.int32)
        receivers = jax.random.randint(ks[3], (N_EDGES,), 0, N_NODES, dtype=jnp.int32)
        W1 = jax.random.normal(ks[4], (IN_F, HIDDEN), dtype=jnp.float32) / np.sqrt(IN_F)
        b1 = jnp.zeros((HIDDEN,), dtype=jnp.float32)
        W2 = jax.random.normal(ks[5], (HIDDEN, OUT_F), dtype=jnp.float32) / np.sqrt(HIDDEN)
        b2 = jnp.zeros((OUT_F,), dtype=jnp.float32)
        Wn = jax.random.normal(ks[6], (NODE_F, OUT_F), dtype=jnp.float32) / np.sqrt(NODE_F)
        bn = jnp.zeros((OUT_F,), dtype=jnp.float32)
        return {'nodes': nodes, 'edges': edges, 'senders': senders, 'receivers': receivers, 'W1': W1, 'b1': b1, 'W2': W2, 'b2': b2, 'Wn': Wn, 'bn': bn}
    _L0_gnn_all = _L0_gnn_setup()
    _L0_gnn_in = {k: v for k, v in _L0_gnn_all.items() if k in ('W1', 'b1', 'W2', 'b2', 'Wn', 'bn')}
    del _L0_gnn_all

    def _L1_gnn_setup():
        import jax, jax.numpy as jnp
        import numpy as np
        N, E, D_IN, D_OUT, R = (6250, 100000, 64, 64, 32)
        key = jax.random.key(seed)
        k = jax.random.split(key, 8)
        feat = jax.random.normal(k[0], (N, D_IN), dtype=jnp.float32)
        src = jax.random.randint(k[1], (E,), 0, N)
        dst = jax.random.randint(k[2], (E,), 0, N)
        etypes = jax.random.randint(k[3], (E,), 0, R)
        norm = jax.random.uniform(k[4], (E, 1), dtype=jnp.float32)
        W = jax.random.normal(k[5], (R, D_IN, D_OUT), dtype=jnp.float32) * (1.0 / np.sqrt(D_IN))
        gain = np.sqrt(2.0)
        bound = gain * np.sqrt(6.0 / (D_IN + D_OUT))
        loop_weight = jax.random.uniform(k[6], (D_IN, D_OUT), dtype=jnp.float32, minval=-bound, maxval=bound)
        h_bias = jnp.zeros((D_OUT,), dtype=jnp.float32)
        return {'feat': feat, 'src': src, 'dst': dst, 'etypes': etypes, 'norm': norm, 'W': W, 'loop_weight': loop_weight, 'h_bias': h_bias}
    _L1_gnn_all = _L1_gnn_setup()
    _L1_gnn_in = {k: v for k, v in _L1_gnn_all.items() if k in ('W', 'loop_weight', 'h_bias')}
    del _L1_gnn_all
    return {'x': x, 'src': src, 'dst': dst, 'edge_attr_32': edge_attr_32, 'edge_type_32': edge_type_32, 'edge_weight1': edge_weight1, 'L0_gnn_W1': _L0_gnn_in['W1'], 'L0_gnn_b1': _L0_gnn_in['b1'], 'L0_gnn_W2': _L0_gnn_in['W2'], 'L0_gnn_b2': _L0_gnn_in['b2'], 'L0_gnn_Wn': _L0_gnn_in['Wn'], 'L0_gnn_bn': _L0_gnn_in['bn'], 'L1_gnn_W': _L1_gnn_in['W'], 'L1_gnn_loop_weight': _L1_gnn_in['loop_weight'], 'L1_gnn_h_bias': _L1_gnn_in['h_bias']}

def reference(x, src, dst, edge_attr_32, edge_type_32, edge_weight1, L0_gnn_W1, L0_gnn_b1, L0_gnn_W2, L0_gnn_b2, L0_gnn_Wn, L0_gnn_bn, L1_gnn_W, L1_gnn_loop_weight, L1_gnn_h_bias):
    import jax
    import jax.numpy as jnp

    def _L0_gnn_ref(nodes, edges, senders, receivers, W1, b1, W2, b2, Wn, bn):
        import jax, jax.numpy as jnp
        import numpy as np
        N_NODES = 12500
        N_EDGES = 200000
        NODE_F = 64
        EDGE_F = 32
        OUT_F = 64
        HIDDEN = 2 * OUT_F
        IN_F = 2 * NODE_F + EDGE_F
        n_nodes = nodes.shape[0]
        sender_features = nodes[senders]
        receiver_features = nodes[receivers]
        concat = jnp.concatenate([sender_features, receiver_features, edges], axis=-1)
        h = jax.nn.relu(concat @ W1 + b1)
        messages = h @ W2 + b2
        aggregated = jax.ops.segment_sum(messages, receivers, num_segments=n_nodes)
        degree = jax.ops.segment_sum(jnp.ones((receivers.shape[0],), dtype=messages.dtype), receivers, num_segments=n_nodes)
        aggregated = aggregated / jnp.maximum(degree, 1.0)[:, None]
        new_nodes = aggregated + (nodes @ Wn + bn)
        return new_nodes

    def _L1_gnn_ref(feat, src, dst, etypes, norm, W, loop_weight, h_bias):
        import jax, jax.numpy as jnp
        import numpy as np
        N, E, D_IN, D_OUT, R = (6250, 100000, 64, 64, 32)
        n_nodes = feat.shape[0]
        proj = jnp.einsum('nd,rdo->nro', feat, W)
        msg = proj[src, etypes] * norm
        h = jax.ops.segment_sum(msg, dst, num_segments=n_nodes)
        h = h + h_bias
        h = h + feat @ loop_weight
        return h
    h = jnp.maximum(_layernorm(x, axis=-1), 0.0)
    x = x + _L0_gnn_ref(h, edge_attr_32, src, dst, L0_gnn_W1, L0_gnn_b1, L0_gnn_W2, L0_gnn_b2, L0_gnn_Wn, L0_gnn_bn)
    h = jnp.maximum(_layernorm(x, axis=-1), 0.0)
    x = x + _L1_gnn_ref(h, src, dst, edge_type_32, edge_weight1, L1_gnn_W, L1_gnn_loop_weight, L1_gnn_h_bias)
    return x

_drawn_inputs = setup_inputs


def setup_inputs(seed=0):
    import zlib

    import numpy as np

    out = dict(_drawn_inputs(seed))
    spreads = {'L0_gnn_b1': (0.0, 0.1),
     'L0_gnn_b2': (0.0, 0.1),
     'L0_gnn_bn': (0.0, 0.1),
     'L1_gnn_h_bias': (0.0, 0.1)}
    factors = {}
    for name, (base, spread) in spreads.items():
        noise = np.random.default_rng([zlib.crc32(name.encode()), seed]).standard_normal(out[name].shape)
        drawn = base * np.exp(spread * noise) if base else spread * noise
        out[name] = jnp.asarray(drawn.astype(out[name].dtype))
    for name, factor in factors.items():
        out[name] = (out[name] * factor).astype(out[name].dtype)
    return out
```

```python
import numpy as np
import concourse.bass as bass
from concourse import mybir
from contextlib import ExitStack

P = 128
NODES, FEAT, HID, EDGE_F, TYPES = 12500, 64, 128, 32, 32
EDGES = 212500
TILES_PER_MACRO = 8
MACRO = P * TILES_PER_MACRO
MACROS = -(-EDGES // MACRO)
TILES = MACROS * TILES_PER_MACRO
EDGES_PAD = MACROS * MACRO
WINDOW = P - EDGE_F
CHUNK_BLOCKS, GROUP_BLOCKS = 9, 3
GROUPS = CHUNK_BLOCKS // GROUP_BLOCKS
BLOCKS = -(-(-(-(NODES + WINDOW) // P)) // CHUNK_BLOCKS) * CHUNK_BLOCKS
CHUNKS = BLOCKS // CHUNK_BLOCKS
NODES_PAD = BLOCKS * P
CHUNK_NODES = CHUNK_BLOCKS * P
CHUNK_COLS = CHUNK_BLOCKS * FEAT
GROUP_COLS = GROUP_BLOCKS * FEAT
PROJ = TYPES * FEAT
EPS = 1e-5


def gnn_kernel(nc, x_in, src_in, type_in, norm_in, dst_in, dst_row, dst_first, edges_t, w_pre_in,
               w_edge_in, w2_in, b2_in, w_proj_in, ident_in, window_row, window_col, out):
    f32, i32 = mybir.dt.float32, mybir.dt.int32
    ALU, ACT, AX = mybir.AluOpType, mybir.ActivationFunctionType, mybir.AxisListType

    p_table = nc.dram_tensor("p_table", [NODES_PAD, HID], f32, kind="Internal").ap()
    q_table = nc.dram_tensor("q_table", [NODES_PAD, HID], f32, kind="Internal").ap()
    proj_table = nc.dram_tensor("proj_table", [NODES_PAD, PROJ], f32, kind="Internal").ap()
    p_rows = p_table.rearrange("(b p) f -> p b f", p=P)
    q_rows = q_table.rearrange("(b p) f -> p b f", p=P)
    proj_rows = proj_table.rearrange("(b p) f -> p b f", p=P)
    proj_by_type = proj_table.rearrange("n (r f) -> (n r) f", f=FEAT)

    keep = ExitStack()
    with keep:
        def buffer(where, name, shape, dt=f32):
            return where.enter_context(nc.sbuf_tensor(name, shape, dt))

        def bank(where, name, shape):
            return where.enter_context(nc.psum_tensor(name, shape, f32))

        def signal(where, name):
            return where.enter_context(nc.semaphore(name))

        x_sb = buffer(keep, "x_sb", [P, BLOCKS * FEAT])
        acc = buffer(keep, "acc", [P, NODES_PAD])
        acc1 = buffer(keep, "acc1", [FEAT + 1, NODES_PAD])
        degree = acc1[FEAT:FEAT + 1, :]
        src_sb = buffer(keep, "src_sb", [P, TILES], i32)
        src_type = buffer(keep, "src_type", [P, TILES], i32)
        norm_sb = buffer(keep, "norm_sb", [P, TILES])
        local_dst = buffer(keep, "local_dst", [P, TILES])
        first_sb = buffer(keep, "first_sb", [P, MACROS], i32)
        window_ids = buffer(keep, "window_ids", [P, MACROS])
        window_row_sb = buffer(keep, "window_row_sb", [P, WINDOW])
        ident = buffer(keep, "ident", [P, P])

        with ExitStack() as s:
            centred = buffer(s, "centred", [P, CHUNK_COLS])
            squares = buffer(s, "squares", [P, CHUNK_COLS])
            stats = buffer(s, "stats", [P, 5, CHUNK_BLOCKS])
            h = buffer(s, "h", [P, CHUNK_COLS])
            h_t = buffer(s, "h_t", [FEAT + 1, GROUPS, GROUP_BLOCKS * P])
            w_pre = buffer(s, "w_pre", [FEAT + 1, 2 * HID + FEAT])
            staged = buffer(s, "staged", [P, GROUPS, GROUP_BLOCKS, 2 * HID])
            dst_sb = buffer(s, "dst_sb", [P, TILES], i32)
            type_sb = buffer(s, "type_sb", [P, TILES], i32)
            window_col_sb = buffer(s, "window_col_sb", [P, 1])
            ps_t = [bank(s, f"ps_t{g}", [P, 512]) for g in range(2)]
            ps_pq = [bank(s, f"ps_pq{b}", [P, 512]) for b in range(GROUP_BLOCKS)]
            ps_self = [bank(s, f"ps_self{g}", [P, 512]) for g in range(2)]
            x_loaded, tables_loaded = signal(s, "x_loaded"), signal(s, "tables_loaded")
            step, var_ready, root_ready = signal(s, "step"), signal(s, "var_ready"), signal(s, "root_ready")
            h_ready, h_read = signal(s, "h_ready"), signal(s, "h_read")
            transposed, copied = signal(s, "transposed"), signal(s, "copied")
            pq_ready, pq_copied = signal(s, "pq_ready"), signal(s, "pq_copied")
            self_ready, self_added = signal(s, "self_ready"), signal(s, "self_added")
            staging_free = signal(s, "staging_free")
            turned = signal(s, "turned")
            ones_set, cleared = signal(s, "ones_set"), signal(s, "cleared")
            stored = [signal(s, f"stored{g}") for g in range(GROUPS)]
            block = s.enter_context(nc.Block())

            @block.sync
            def _(sp):
                sp.dma_start(x_sb[:], x_in).then_inc(x_loaded, 16)
                sp.dma_start(w_pre[:], w_pre_in).then_inc(x_loaded, 16)
                sp.dma_start(ident[:], ident_in).then_inc(x_loaded, 16)
                for to, of in ((src_sb, src_in), (type_sb, type_in), (norm_sb, norm_in), (dst_sb, dst_in),
                               (window_col_sb, window_col), (window_row_sb, window_row.partition_broadcast(P)[:, 0, :]),
                               (first_sb, dst_first.partition_broadcast(P)[:, 0, :])):
                    sp.dma_start(to[:], of).then_inc(tables_loaded, 16)
                sp.sem_inc(staging_free, GROUPS)
                with sp.Fori(0, CHUNKS) as c:
                    for g in range(GROUPS):
                        sp.wait_ge(pq_copied, c * CHUNK_BLOCKS + (g + 1) * GROUP_BLOCKS + GROUP_BLOCKS)
                        rows = bass.ds(c * CHUNK_BLOCKS + g * GROUP_BLOCKS, GROUP_BLOCKS)
                        sp.dma_start(p_rows[:, rows, :], staged[:, g, :, 0:HID]).then_inc(stored[g], 16)
                        sp.dma_start(q_rows[:, rows, :], staged[:, g, :, HID:2 * HID]).then_inc(stored[g], 16)
                        if g > 0:
                            sp.wait_ge(stored[g - 1], c * 32 + 32)
                            sp.sem_inc(staging_free, 1)
                    sp.wait_ge(stored[GROUPS - 1], c * 32 + 32)
                    sp.sem_inc(staging_free, 1)

            @block.gpsimd
            def _(pool):
                pool.memset(acc[:], 0.0).then_inc(cleared, 1)
                pool.memset(acc1[:], 0.0).then_inc(cleared, 1)

            @block.vector
            def _(dve):
                dve.sem_inc(self_added, GROUPS)
                dve.sem_inc(h_read, 1)
                dve.memset(h_t[FEAT:FEAT + 1, :, :], 1.0).then_inc(ones_set, 1)
                dve.wait_ge(x_loaded, 48)
                dve.wait_ge(tables_loaded, 7 * 16)
                dve.tensor_scalar(window_ids[:], first_sb[:], window_col_sb[:, 0:1], None, ALU.add)
                per_tile = first_sb[:].unsqueeze(2).to_broadcast([P, MACROS, TILES_PER_MACRO])
                dve.tensor_tensor(local_dst[:].rearrange("p (m t) -> p m t", t=TILES_PER_MACRO),
                                  dst_sb[:].rearrange("p (m t) -> p m t", t=TILES_PER_MACRO), per_tile, ALU.subtract)
                dve.scalar_tensor_tensor(src_type[:], src_sb[:], float(TYPES), type_sb[:], ALU.mult, ALU.add)
                steps = 7
                with dve.Fori(0, CHUNKS) as c:
                    xv = x_sb[:, bass.ds(c * CHUNK_COLS, CHUNK_COLS)].rearrange("p (b f) -> p b f", f=FEAT)
                    cv = centred[:].rearrange("p (b f) -> p b f", f=FEAT)
                    sv = squares[:].rearrange("p (b f) -> p b f", f=FEAT)
                    wide = [P, CHUNK_BLOCKS, FEAT]
                    dve.tensor_reduce(stats[:, 0, :], xv, AX.X, ALU.add).then_inc(step, 1)
                    dve.wait_ge(step, c * steps + 1)
                    dve.tensor_scalar(stats[:, 1, :], stats[:, 0, :], -1.0 / FEAT, None, ALU.mult).then_inc(step, 1)
                    dve.wait_ge(step, c * steps + 2)
                    dve.tensor_tensor(cv, xv, stats[:, 1, :].unsqueeze(2).to_broadcast(wide), ALU.add).then_inc(step, 1)
                    dve.wait_ge(step, c * steps + 3)
                    dve.tensor_tensor(sv, cv, cv, ALU.mult).then_inc(step, 1)
                    dve.wait_ge(step, c * steps + 4)
                    dve.tensor_reduce(stats[:, 2, :], sv, AX.X, ALU.add).then_inc(step, 1)
                    dve.wait_ge(step, c * steps + 5)
                    dve.tensor_scalar(stats[:, 3, :], stats[:, 2, :], 1.0 / FEAT, EPS, ALU.mult, ALU.add).then_inc(var_ready, 1)
                    dve.wait_ge(root_ready, c + 1)
                    dve.reciprocal(stats[:, 4, :], stats[:, 3, :]).then_inc(step, 1)
                    dve.wait_ge(step, c * steps + 6)
                    dve.wait_ge(h_read, c + 1)
                    dve.scalar_tensor_tensor(h[:].rearrange("p (b f) -> p b f", f=FEAT), cv, 0.0,
                                             stats[:, 4, :].unsqueeze(2).to_broadcast(wide),
                                             ALU.max, ALU.mult).then_inc(h_ready, 1)
                    dve.wait_ge(h_ready, c + 1)
                    dve.tensor_copy(stats[:, 0, 0:1], stats[:, 0, 0:1]).then_inc(step, 1)
                    dve.wait_ge(step, c * steps + 7)
                    for g in range(GROUPS):
                        dve.wait_ge(self_ready, c * GROUPS + g + 1)
                        xg = x_sb[:, bass.ds(c * CHUNK_COLS + g * GROUP_COLS, GROUP_COLS)]
                        dve.tensor_tensor(xg, xg, ps_self[g % 2][:, 0:GROUP_COLS], ALU.add).then_inc(self_added, 1)

            @block.scalar
            def _(act):
                act.sem_inc(pq_copied, GROUP_BLOCKS)
                with act.Fori(0, CHUNKS) as c:
                    act.wait_ge(var_ready, c + 1)
                    act.activation(stats[:, 3, :], stats[:, 3, :], ACT.Sqrt).then_inc(root_ready, 1)

                    def copy_transposed(g):
                        act.wait_ge(transposed, c * GROUPS + g + 1)
                        act.activation(h_t[0:FEAT, g, :], ps_t[g % 2][0:FEAT, 0:GROUP_BLOCKS * P],
                                       ACT.Copy).then_inc(copied, 1)

                    def stage(g):
                        act.wait_ge(staging_free, c * GROUPS + g + 1)
                        for b in range(GROUP_BLOCKS):
                            act.wait_ge(pq_ready, c * CHUNK_BLOCKS + g * GROUP_BLOCKS + b + 1)
                            act.activation(staged[:, g, b, :], ps_pq[b][:, 0:2 * HID], ACT.Copy).then_inc(pq_copied, 1)

                    copy_transposed(0)
                    copy_transposed(1)
                    stage(0)
                    copy_transposed(2)
                    stage(1)
                    stage(2)

            @block.tensor
            def _(pe):
                pe.wait_ge(x_loaded, 48)
                pe.wait_ge(ones_set, 1)
                with pe.Fori(0, CHUNKS) as c:
                    pe.wait_ge(h_ready, c + 1)
                    pe.sem_inc(turned, 1)

                    def transpose(g):
                        for b in range(GROUP_BLOCKS):
                            col = (g * GROUP_BLOCKS + b) * FEAT
                            last = pe.transpose(ps_t[g % 2][0:FEAT, b * P:(b + 1) * P], h[:, col:col + FEAT], ident[:])
                        last.then_inc(transposed, 1)

                    def products(g):
                        pe.wait_ge(copied, c * GROUPS + g + 1)
                        for b in range(GROUP_BLOCKS):
                            pe.wait_ge(pq_copied, c * CHUNK_BLOCKS + g * GROUP_BLOCKS + b + 1)
                            pe.matmul(ps_pq[b][:, 0:2 * HID], h_t[:, g, b * P:(b + 1) * P], w_pre[:, 0:2 * HID],
                                      start=True, stop=True).then_inc(pq_ready, 1)
                        pe.wait_ge(self_added, c * GROUPS + (GROUPS, 2, 4)[g])
                        for b in range(GROUP_BLOCKS):
                            last = pe.matmul(ps_self[g % 2][:, b * FEAT:(b + 1) * FEAT], h_t[:, g, b * P:(b + 1) * P],
                                             w_pre[:, 2 * HID:], start=True, stop=True)
                        last.then_inc(self_ready, 1)

                    transpose(0)
                    transpose(1)
                    products(0)
                    transpose(2)
                    products(1)
                    pe.wait_ge(copied, c * GROUPS + GROUPS)
                    pe.sem_inc(h_read, 1)
                    products(2)

        with ExitStack() as s:
            stack = buffer(s, "stack", [P, 2, MACRO])
            window_q = buffer(s, "window_q", [P, 2, HID])
            dst_wide = buffer(s, "dst_wide", [WINDOW, 2, MACRO], i32)
            one_hot = buffer(s, "one_hot", [P, 2, TILES_PER_MACRO, WINDOW])
            gathered = buffer(s, "gathered", [P, 2, 2, 4 * HID])
            index = buffer(s, "index", [P, 2, TILES_PER_MACRO], i32)
            ones = buffer(s, "ones", [P, P])
            ps_pre = [bank(s, f"ps_pre{k}", [P, 512]) for k in range(2)]
            ps_acc = [bank(s, f"ps_acc{k}", [P, 512]) for k in range(2)]
            ps_deg = [bank(s, f"ps_deg{k}", [P, 512]) for k in range(2)]
            w_loaded, ones_ready = signal(s, "w_loaded"), signal(s, "ones_ready")
            begun = signal(s, "begun")
            operands = [signal(s, f"operands{k}") for k in range(2)]
            dst_loaded = [signal(s, f"dst_loaded{k}") for k in range(2)]
            index_loaded = [signal(s, f"index_loaded{k}") for k in range(2)]
            landed = [[signal(s, f"landed{k}{f}") for f in range(2)] for k in range(2)]
            spread, hot_ready = signal(s, "spread"), signal(s, "hot_ready")
            pre_ready, summed, relu_done = signal(s, "pre_ready"), signal(s, "summed"), signal(s, "relu_done")
            half_used, sums_ready = signal(s, "half_used"), signal(s, "sums_ready")
            sums_added, acc_step = signal(s, "sums_added"), signal(s, "acc_step")
            block = s.enter_context(nc.Block())
            HALVES = 4

            @block.sync
            def _(sp):
                sp.sem_inc(spread, 2)
                sp.sem_inc(half_used, HALVES)
                sp.sem_inc(pre_ready, HALVES)
                sp.sem_inc(summed, 2)
                sp.sem_inc(sums_added, 2)
                for k in range(2):
                    sp.dma_start(window_q[WINDOW:P, k, :], w_edge_in).then_inc(w_loaded, 16)
                with sp.Fori(0, MACROS // 2) as i:
                    for k in range(2):
                        m = i * 2 + k
                        first = sp.value_load(first_sb[0:1, bass.ds(m, 1)], min_val=0, max_val=NODES - 1)
                        sp.wait_ge(half_used, m * 2 + 2)
                        sp.dma_start(index[:, k, :], src_sb[:, bass.ds(m * TILES_PER_MACRO, TILES_PER_MACRO)]
                                     ).then_inc(index_loaded[k], 16)
                        sp.wait_ge(spread, m + 1)
                        sp.dma_start(dst_wide[:, k, :], dst_row[0:1, bass.ds(m * MACRO, MACRO)].partition_broadcast(WINDOW)[:, 0, :]
                                     ).then_inc(dst_loaded[k], 16)
                        sp.wait_ge(pre_ready, m * 2 + 2)
                        sp.dma_start(stack[WINDOW:P, k, :], edges_t[:, bass.ds(m * MACRO, MACRO)]).then_inc(operands[k], 16)
                        sp.dma_start(window_q[0:WINDOW, k, :], q_table[bass.ds(first, WINDOW), :]).then_inc(operands[k], 16)

            @block.gpsimd
            def _(pool):
                with pool.Fori(0, MACROS // 2) as i:
                    for k in range(2):
                        pool.wait_ge(index_loaded[k], i * 16 + 16)
                        for f in range(2):
                            pool.wait_ge(half_used, i * 4 + (k * 2 + f + 1))
                            pool.sem_inc(begun, 1)
                            for j in range(4):
                                pool.indirect_dma_start(
                                    out=gathered[:, k, f, j * HID:(j + 1) * HID], out_offset=None, in_=p_table,
                                    in_offset=bass.IndirectOffsetOnAxis(ap=index[:, k, 4 * f + j:4 * f + j + 1], axis=0)
                                ).then_inc(landed[k][f], 16)

            @block.vector
            def _(dve):
                dve.memset(ones[:], 1.0).then_inc(ones_ready, 1)
                with dve.Fori(0, MACROS // 2) as i:
                    def spread_out(k):
                        m = i * 2 + k
                        dve.wait_ge(dst_loaded[k], i * 16 + 16)
                        dve.wait_ge(pre_ready, m * 2 + 2)
                        dve.tensor_scalar(stack[0:WINDOW, k, :], dst_wide[:, k, :], window_ids[0:WINDOW, bass.ds(m, 1)],
                                          None, ALU.is_equal).then_inc(spread, 1)
                        dve.wait_ge(half_used, m * 2 + 2)
                        for t in range(TILES_PER_MACRO):
                            last = dve.tensor_scalar(one_hot[:, k, t, :], window_row_sb[:],
                                                     local_dst[:, bass.ds(m * TILES_PER_MACRO + t, 1)], None, ALU.is_equal)
                        last.then_inc(hot_ready, 1)

                    def add_gathered(k, f):
                        m = i * 2 + k
                        dve.wait_ge(pre_ready, m * 2 + (f + 1) + HALVES)
                        dve.wait_ge(landed[k][f], i * 64 + 64)
                        half = gathered[:, k, f, :]
                        dve.tensor_tensor(half, ps_pre[f][:], half, ALU.add).then_inc(summed, 1)

                    def accumulate(k):
                        m = i * 2 + k
                        first = dve.value_load(first_sb[0:1, bass.ds(m, 1)], min_val=0, max_val=NODES - 1)
                        dve.wait_ge(sums_ready, m + 1)
                        dve.wait_ge(sums_added, m + 2)
                        to = degree[:, bass.ds(first, WINDOW)]
                        dve.tensor_tensor(to, to, ps_deg[k][0:1, 0:WINDOW], ALU.add).then_inc(acc_step, 1)
                        dve.wait_ge(acc_step, m + 1)
                        to = acc[:, bass.ds(first, WINDOW)]
                        dve.tensor_tensor(to, to, ps_acc[k][:, 0:WINDOW], ALU.add).then_inc(sums_added, 1)

                    spread_out(0)
                    add_gathered(0, 0)
                    spread_out(1)
                    add_gathered(0, 1)
                    add_gathered(1, 0)
                    accumulate(0)
                    add_gathered(1, 1)
                    accumulate(1)

            @block.scalar
            def _(act):
                with act.Fori(0, MACROS // 2) as i:
                    for k in range(2):
                        for f in range(2):
                            act.wait_ge(summed, i * 4 + (k * 2 + f + 1) + 2)
                            half = gathered[:, k, f, :]
                            act.activation(half, half, ACT.Relu).then_inc(relu_done, 1)

            @block.tensor
            def _(pe):
                pe.wait_ge(w_loaded, 32)
                pe.wait_ge(ones_ready, 1)
                with pe.Fori(0, MACROS // 2) as i:
                    def pre(k, f):
                        m = i * 2 + k
                        if f == 0:
                            pe.wait_ge(operands[k], i * 32 + 32)
                            pe.wait_ge(spread, m + 3)
                        pe.wait_ge(summed, m * 2 + (f + 1))
                        for j in range(4):
                            col = (4 * f + j) * P
                            last = pe.matmul(ps_pre[f][:, j * HID:(j + 1) * HID], stack[:, k, col:col + P],
                                             window_q[:, k, :], start=True, stop=True)
                        last.then_inc(pre_ready, 1)

                    def sums(k, f):
                        m = i * 2 + k
                        if f == 0:
                            pe.wait_ge(hot_ready, m + 1)
                            pe.wait_ge(sums_added, m + 1)
                        for j in range(4):
                            t = 4 * f + j
                            last_deg = pe.matmul(ps_deg[k][:, 0:WINDOW], ones[:], one_hot[:, k, t, :],
                                                 start=(t == 0), stop=(t == TILES_PER_MACRO - 1))
                        pe.wait_ge(relu_done, m * 2 + (f + 1))
                        for j in range(4):
                            t = 4 * f + j
                            last = pe.matmul(ps_acc[k][:, 0:WINDOW], gathered[:, k, f, j * HID:(j + 1) * HID],
                                             one_hot[:, k, t, :], start=(t == 0), stop=(t == TILES_PER_MACRO - 1))
                        last.then_inc(half_used, 1)
                        if f == 1:
                            pe.wait_ge(half_used, m * 2 + 2 + HALVES)
                            pe.sem_inc(sums_ready, 1)

                    pre(0, 0)
                    pre(0, 1)
                    sums(0, 0)
                    pre(1, 0)
                    sums(0, 1)
                    pre(1, 1)
                    sums(1, 0)
                    sums(1, 1)

        with ExitStack() as s:
            acc_now = buffer(s, "acc_now", [P, CHUNK_NODES])
            degree_now = buffer(s, "degree_now", [1, CHUNK_NODES])
            x_now = buffer(s, "x_now", [P, CHUNK_COLS])
            centred = buffer(s, "centred_1", [P, CHUNK_COLS])
            squares = buffer(s, "squares_1", [P, CHUNK_COLS])
            stats = buffer(s, "stats_1", [P, 5, CHUNK_BLOCKS])
            h = buffer(s, "h_1", [P, CHUNK_COLS])
            h_t = buffer(s, "h_t_1", [FEAT + 1, 2, GROUP_BLOCKS * P])
            w2 = buffer(s, "w2", [HID, FEAT + 1])
            b2 = buffer(s, "b2", [1, FEAT + 1])
            w_proj = buffer(s, "w_proj", [FEAT + 1, PROJ + FEAT])
            inverse = buffer(s, "inverse", [P, 2, GROUP_BLOCKS])
            staged = buffer(s, "staged_1", [P, GROUP_BLOCKS, PROJ])
            ps_t = bank(s, "ps_t_1", [P, 512])
            ps_mean = bank(s, "ps_mean", [P, 512])
            ps_self = bank(s, "ps_self_1", [P, 512])
            ps_proj = [bank(s, f"ps_proj{q}", [P, 512]) for q in range(4)]
            w_loaded = signal(s, "w_loaded_1")
            acc_copied, deg_copied = signal(s, "acc_copied"), signal(s, "deg_copied")
            ones_set, step = signal(s, "ones_set_1"), signal(s, "step_1")
            mean_ready, mean_read = signal(s, "mean_ready"), signal(s, "mean_read")
            var_ready, root_ready, h_ready = signal(s, "var_ready_1"), signal(s, "root_ready_1"), signal(s, "h_ready_1")
            transposed, copied = signal(s, "transposed_1"), signal(s, "copied_1")
            left_ready, left_copied = signal(s, "left_ready"), signal(s, "left_copied")
            right_ready, right_copied = signal(s, "right_ready"), signal(s, "right_copied")
            self_ready, self_added = signal(s, "self_ready_1"), signal(s, "self_added_1")
            slot_free = signal(s, "slot_free")
            turned = signal(s, "turned_1")
            stored = [signal(s, f"stored_1{b}") for b in range(GROUP_BLOCKS)]
            block = s.enter_context(nc.Block())

            @block.sync
            def _(sp):
                for to, of in ((w2, w2_in), (b2, b2_in), (w_proj, w_proj_in)):
                    sp.dma_start(to[:], of).then_inc(w_loaded, 16)
                sp.sem_inc(slot_free, GROUP_BLOCKS)
                sp.sem_inc(mean_read, 1)
                sp.sem_inc(self_added, 1)
                with sp.Fori(0, BLOCKS // GROUP_BLOCKS) as n:
                    for b in range(GROUP_BLOCKS):
                        sp.wait_ge(left_copied, n * GROUP_BLOCKS + (b + 2))
                        sp.wait_ge(right_copied, n * GROUP_BLOCKS + (b + 2))
                        sp.dma_start(proj_rows[:, bass.ds(n * GROUP_BLOCKS + b, 1), :], staged[:, b:b + 1, :]
                                     ).then_inc(stored[b], 16)
                        if b > 0:
                            sp.wait_ge(stored[b - 1], n * 16 + 16)
                            sp.sem_inc(slot_free, 1)
                    sp.wait_ge(stored[GROUP_BLOCKS - 1], n * 16 + 16)
                    sp.sem_inc(slot_free, 1)

            @block.vector
            def _(dve):
                dve.sem_inc(right_copied, 1)
                dve.memset(h_t[FEAT:FEAT + 1, :, :], 1.0).then_inc(ones_set, 1)
                steps = 6 + 3 * GROUPS
                with dve.Fori(0, CHUNKS) as c:
                    count = [0]

                    def link(instruction):
                        instruction.then_inc(step, 1)
                        count[0] += 1
                        dve.wait_ge(step, c * steps + count[0])

                    wide = [P, CHUNK_BLOCKS, FEAT]
                    for g in range(GROUPS):
                        dve.wait_ge(mean_ready, c * GROUPS + g + 1)
                        mean = ps_mean[:, 0:GROUP_BLOCKS * (FEAT + 1)].rearrange("p (b f) -> p b f", f=FEAT + 1)
                        link(dve.tensor_scalar(inverse[:, 0, :], mean[:, :, FEAT], 1.0, None, ALU.max))
                        link(dve.reciprocal(inverse[:, 1, :], inverse[:, 0, :]))
                        cg = centred[:, g * GROUP_COLS:(g + 1) * GROUP_COLS].rearrange("p (b f) -> p b f", f=FEAT)
                        dve.tensor_tensor(cg, mean[:, :, 0:FEAT],
                                          inverse[:, 1, :].unsqueeze(2).to_broadcast([P, GROUP_BLOCKS, FEAT]),
                                          ALU.mult).then_inc(mean_read, 1)
                        dve.wait_ge(mean_read, c * GROUPS + g + 2)
                        xg = x_sb[:, bass.ds(c * CHUNK_COLS + g * GROUP_COLS, GROUP_COLS)]
                        link(dve.tensor_tensor(x_now[:, g * GROUP_COLS:(g + 1) * GROUP_COLS], xg,
                                               centred[:, g * GROUP_COLS:(g + 1) * GROUP_COLS], ALU.add))
                    xv = x_now[:].rearrange("p (b f) -> p b f", f=FEAT)
                    cv = centred[:].rearrange("p (b f) -> p b f", f=FEAT)
                    sv = squares[:].rearrange("p (b f) -> p b f", f=FEAT)
                    link(dve.tensor_reduce(stats[:, 0, :], xv, AX.X, ALU.add))
                    link(dve.tensor_scalar(stats[:, 1, :], stats[:, 0, :], -1.0 / FEAT, None, ALU.mult))
                    link(dve.tensor_tensor(cv, xv, stats[:, 1, :].unsqueeze(2).to_broadcast(wide), ALU.add))
                    link(dve.tensor_tensor(sv, cv, cv, ALU.mult))
                    link(dve.tensor_reduce(stats[:, 2, :], sv, AX.X, ALU.add))
                    dve.tensor_scalar(stats[:, 3, :], stats[:, 2, :], 1.0 / FEAT, EPS, ALU.mult, ALU.add).then_inc(var_ready, 1)
                    dve.wait_ge(root_ready, c + 1)
                    link(dve.reciprocal(stats[:, 4, :], stats[:, 3, :]))
                    assert count[0] == steps
                    dve.scalar_tensor_tensor(h[:].rearrange("p (b f) -> p b f", f=FEAT), cv, 0.0,
                                             stats[:, 4, :].unsqueeze(2).to_broadcast(wide),
                                             ALU.max, ALU.mult).then_inc(h_ready, 1)
                    dve.wait_ge(h_ready, c + 1)
                    for g in range(GROUPS):
                        for b in range(GROUP_BLOCKS):
                            n = c * CHUNK_BLOCKS + g * GROUP_BLOCKS + b
                            dve.wait_ge(slot_free, n + 1)
                            dve.wait_ge(right_ready, n + 1)
                            for q in (2, 3):
                                last = dve.tensor_copy(staged[:, b, q * 512:(q + 1) * 512], ps_proj[q][:])
                            last.then_inc(right_copied, 1)
                        dve.wait_ge(self_ready, c * GROUPS + g + 1)
                        xg = x_sb[:, bass.ds(c * CHUNK_COLS + g * GROUP_COLS, GROUP_COLS)]
                        dve.tensor_tensor(xg, x_now[:, g * GROUP_COLS:(g + 1) * GROUP_COLS], ps_self[:, 0:GROUP_COLS],
                                          ALU.add).then_inc(self_added, 1)

            @block.scalar
            def _(act):
                act.sem_inc(left_copied, 1)
                with act.Fori(0, CHUNKS) as c:
                    act.activation(acc_now[:], acc[:, bass.ds(c * CHUNK_NODES, CHUNK_NODES)], ACT.Copy).then_inc(acc_copied, 1)
                    act.activation(degree_now[:], degree[:, bass.ds(c * CHUNK_NODES, CHUNK_NODES)], ACT.Copy).then_inc(deg_copied, 1)
                    act.wait_ge(var_ready, c + 1)
                    act.activation(stats[:, 3, :], stats[:, 3, :], ACT.Sqrt).then_inc(root_ready, 1)

                    def copy_transposed(g):
                        act.wait_ge(transposed, c * GROUPS + g + 1)
                        act.activation(h_t[0:FEAT, g % 2, :], ps_t[0:FEAT, 0:GROUP_BLOCKS * P],
                                       ACT.Copy).then_inc(copied, 1)

                    copy_transposed(0)
                    for g in range(GROUPS):
                        if g + 1 < GROUPS:
                            copy_transposed(g + 1)
                        for b in range(GROUP_BLOCKS):
                            n = c * CHUNK_BLOCKS + g * GROUP_BLOCKS + b
                            act.wait_ge(slot_free, n + 1)
                            act.wait_ge(left_ready, n + 1)
                            for q in (0, 1):
                                last = act.activation(staged[:, b, q * 512:(q + 1) * 512], ps_proj[q][:], ACT.Copy)
                            last.then_inc(left_copied, 1)

            @block.tensor
            def _(pe):
                pe.wait_ge(w_loaded, 48)
                pe.wait_ge(ones_set, 1)
                with pe.Fori(0, CHUNKS) as c:
                    pe.wait_ge(acc_copied, c + 1)
                    pe.wait_ge(deg_copied, c + 1)
                    for g in range(GROUPS):
                        pe.wait_ge(mean_read, c * GROUPS + g + 1)
                        for b in range(GROUP_BLOCKS):
                            node = (g * GROUP_BLOCKS + b) * P
                            to = ps_mean[:, b * (FEAT + 1):(b + 1) * (FEAT + 1)]
                            pe.matmul(to, acc_now[:, node:node + P], w2[:], start=True, stop=False)
                            last = pe.matmul(to, degree_now[:, node:node + P], b2[:], start=False, stop=True)
                        last.then_inc(mean_ready, 1)
                    pe.wait_ge(h_ready, c + 1)
                    pe.sem_inc(turned, 1)

                    def transpose(g):
                        for b in range(GROUP_BLOCKS):
                            col = (g * GROUP_BLOCKS + b) * FEAT
                            last = pe.transpose(ps_t[0:FEAT, b * P:(b + 1) * P], h[:, col:col + FEAT], ident[:])
                        last.then_inc(transposed, 1)

                    transpose(0)
                    for g in range(GROUPS):
                        pe.wait_ge(copied, c * GROUPS + g + 1)
                        pe.sem_inc(turned, 1)
                        if g + 1 < GROUPS:
                            transpose(g + 1)
                        pe.wait_ge(self_added, c * GROUPS + g + 1)
                        for b in range(GROUP_BLOCKS):
                            last = pe.matmul(ps_self[:, b * FEAT:(b + 1) * FEAT], h_t[:, g % 2, b * P:(b + 1) * P],
                                             w_proj[:, PROJ:], start=True, stop=True)
                        last.then_inc(self_ready, 1)
                        for b in range(GROUP_BLOCKS):
                            n = c * CHUNK_BLOCKS + g * GROUP_BLOCKS + b
                            for half, ready, free in ((0, left_ready, left_copied), (1, right_ready, right_copied)):
                                pe.wait_ge(free, n + 1)
                                for q in (2 * half, 2 * half + 1):
                                    last = pe.matmul(ps_proj[q][:], h_t[:, g % 2, b * P:(b + 1) * P],
                                                     w_proj[:, q * 512:(q + 1) * 512], start=True, stop=True)
                                last.then_inc(ready, 1)

        with ExitStack() as s:
            weighted = buffer(s, "weighted", [P, 2, TILES_PER_MACRO, WINDOW])
            messages = buffer(s, "messages", [P, 2, TILES_PER_MACRO, FEAT])
            index = buffer(s, "index_1", [P, 2, TILES_PER_MACRO], i32)
            ps_sum = [bank(s, f"ps_sum{k}", [P, 512]) for k in range(2)]
            index_loaded = [signal(s, f"index_loaded_1{k}") for k in range(2)]
            landed = [signal(s, f"landed_1{k}") for k in range(2)]
            hot_ready, sums_ready, sums_added = signal(s, "hot_ready_1"), signal(s, "sums_ready_1"), signal(s, "sums_added_1")
            begun = signal(s, "begun_1")
            block = s.enter_context(nc.Block())

            @block.sync
            def _(sp):
                sp.sem_inc(sums_ready, 2)
                sp.sem_inc(sums_added, 2)
                with sp.Fori(0, MACROS // 2) as i:
                    for k in range(2):
                        m = i * 2 + k
                        sp.wait_ge(sums_ready, m + 1)
                        sp.dma_start(index[:, k, :], src_type[:, bass.ds(m * TILES_PER_MACRO, TILES_PER_MACRO)]
                                     ).then_inc(index_loaded[k], 16)

            @block.gpsimd
            def _(pool):
                with pool.Fori(0, MACROS // 2) as i:
                    for k in range(2):
                        pool.wait_ge(index_loaded[k], i * 16 + 16)
                        pool.sem_inc(begun, 1)
                        for t in range(TILES_PER_MACRO):
                            pool.indirect_dma_start(
                                out=messages[:, k, t, :], out_offset=None, in_=proj_by_type,
                                in_offset=bass.IndirectOffsetOnAxis(ap=index[:, k, t:t + 1], axis=0)
                            ).then_inc(landed[k], 16)

            @block.vector
            def _(dve):
                with dve.Fori(0, MACROS // 2) as i:
                    def weigh(k):
                        m = i * 2 + k
                        dve.wait_ge(sums_ready, m + 1)
                        for t in range(TILES_PER_MACRO):
                            tile = bass.ds(m * TILES_PER_MACRO + t, 1)
                            last = dve.tensor_scalar(weighted[:, k, t, :], window_row_sb[:], local_dst[:, tile],
                                                     norm_sb[:, tile], ALU.is_equal, ALU.mult)
                        last.then_inc(hot_ready, 1)

                    def accumulate(k):
                        m = i * 2 + k
                        first = dve.value_load(first_sb[0:1, bass.ds(m, 1)], min_val=0, max_val=NODES - 1)
                        dve.wait_ge(sums_ready, m + 3)
                        dve.wait_ge(sums_added, m + 2)
                        to = acc1[0:FEAT, bass.ds(first, WINDOW)]
                        dve.tensor_tensor(to, to, ps_sum[k][0:FEAT, 0:WINDOW], ALU.add).then_inc(sums_added, 1)

                    weigh(0)
                    weigh(1)
                    accumulate(0)
                    accumulate(1)

            @block.tensor
            def _(pe):
                with pe.Fori(0, MACROS // 2) as i:
                    for k in range(2):
                        m = i * 2 + k
                        pe.wait_ge(hot_ready, m + 1)
                        pe.wait_ge(sums_added, m + 1)
                        pe.wait_ge(landed[k], i * 128 + 128)
                        for t in range(TILES_PER_MACRO):
                            last = pe.matmul(ps_sum[k][0:FEAT, 0:WINDOW], messages[:, k, t, :], weighted[:, k, t, :],
                                             start=(t == 0), stop=(t == TILES_PER_MACRO - 1))
                        last.then_inc(sums_ready, 1)

        with ExitStack() as s:
            acc_now = buffer(s, "acc1_now", [FEAT, 2, CHUNK_NODES])
            ps_out = [bank(s, f"ps_out{g}", [P, 512]) for g in range(GROUPS)]
            chunk_copied, turned, added, stored = (signal(s, n) for n in ("chunk_copied", "turned_2", "added", "out_stored"))
            block = s.enter_context(nc.Block())

            @block.scalar
            def _(act):
                for c in range(CHUNKS):
                    if c >= 2:
                        act.wait_ge(turned, (c - 1) * GROUPS)
                    act.activation(acc_now[:, c % 2, :], acc1[0:FEAT, c * CHUNK_NODES:(c + 1) * CHUNK_NODES],
                                   ACT.Copy).then_inc(chunk_copied, 1)

            @block.tensor
            def _(pe):
                for c in range(CHUNKS):
                    pe.wait_ge(chunk_copied, c + 1)
                    for g in range(GROUPS):
                        if c > 0:
                            pe.wait_ge(added, (c - 1) * GROUPS + g + 1)
                        for b in range(GROUP_BLOCKS):
                            node = (g * GROUP_BLOCKS + b) * P
                            last = pe.transpose(ps_out[g][:, b * FEAT:(b + 1) * FEAT], acc_now[:, c % 2, node:node + P],
                                                ident[0:FEAT, 0:FEAT])
                        last.then_inc(turned, 1)

            @block.vector
            def _(dve):
                for n in range(CHUNKS * GROUPS):
                    dve.wait_ge(turned, n + 1)
                    xg = x_sb[:, n * GROUP_COLS:(n + 1) * GROUP_COLS]
                    dve.tensor_tensor(xg, xg, ps_out[n % GROUPS][:, 0:GROUP_COLS], ALU.add).then_inc(added, 1)

            @block.sync
            def _(sp):
                for c in range(CHUNKS):
                    sp.wait_ge(added, (c + 1) * GROUPS)
                    cols = slice(c * CHUNK_COLS, (c + 1) * CHUNK_COLS)
                    sp.dma_start(out[:, cols], x_sb[:, cols]).then_inc(stored, 16)
                sp.wait_ge(stored, 16 * CHUNKS)


def node_major(a):
    pad = np.zeros((NODES_PAD - NODES, FEAT), a.dtype)
    rows = np.concatenate([a, pad]).reshape(BLOCKS, P, FEAT)
    return np.ascontiguousarray(rows.transpose(1, 0, 2)).reshape(P, BLOCKS * FEAT)


def edge_major(a, pad):
    a = np.concatenate([a.reshape(-1), np.full(EDGES_PAD - EDGES, pad, a.dtype)])
    return np.ascontiguousarray(a.reshape(TILES, P).T)


def kernel(x, src, dst, edge_attr_32, edge_type_32, edge_weight1, L0_gnn_W1, L0_gnn_b1, L0_gnn_W2, L0_gnn_b2,
           L0_gnn_Wn, L0_gnn_bn, L1_gnn_W, L1_gnn_loop_weight, L1_gnn_h_bias):
    import concourse.bacc as bacc
    from concourse.bass_utils import run_bass_kernel_spmd

    (x, src, dst, edge_attr, edge_type, weight, w1, b1, w2, b2, wn, bn, w_rel, w_loop, bias) = (
        np.asarray(a) for a in (x, src, dst, edge_attr_32, edge_type_32, edge_weight1, L0_gnn_W1, L0_gnn_b1, L0_gnn_W2,
                                L0_gnn_b2, L0_gnn_Wn, L0_gnn_bn, L1_gnn_W, L1_gnn_loop_weight, L1_gnn_h_bias))
    f = np.float32
    dst_flat = np.concatenate([dst, np.full(EDGES_PAD - EDGES, -1, dst.dtype)])
    w_pre = np.concatenate([np.concatenate([w1[0:FEAT], w1[FEAT:2 * FEAT], wn], axis=1),
                            np.concatenate([np.zeros(HID, f), b1, bn])[None, :]])
    w_rel = np.ascontiguousarray(w_rel.transpose(1, 0, 2)).reshape(FEAT, PROJ)
    w_proj = np.concatenate([np.concatenate([w_rel, w_loop], axis=1),
                             np.concatenate([np.zeros(PROJ, f), bias])[None, :]])
    arrays = {
        "x_in": node_major(x),
        "src_in": edge_major(src, 0),
        "type_in": edge_major(edge_type, 0),
        "norm_in": edge_major(weight, 0),
        "dst_in": edge_major(dst, -1),
        "dst_row": dst_flat[None, :],
        "dst_first": np.ascontiguousarray(dst_flat[::MACRO])[None, :],
        "edges_t": np.ascontiguousarray(np.concatenate([edge_attr, np.zeros((EDGES_PAD - EDGES, EDGE_F), f)]).T),
        "w_pre_in": w_pre,
        "w_edge_in": np.ascontiguousarray(w1[2 * FEAT:]),
        "w2_in": np.concatenate([w2, np.zeros((HID, 1), f)], axis=1),
        "b2_in": np.concatenate([b2, np.ones(1, f)])[None, :],
        "w_proj_in": w_proj,
        "ident_in": np.eye(P, dtype=f),
        "window_row": np.arange(WINDOW, dtype=f)[None, :],
        "window_col": np.arange(P, dtype=f)[:, None],
    }
    nc = bacc.Bacc("TRN2", target_bir_lowering=False, num_devices=1)
    args = [nc.dram_tensor(n, a.shape, mybir.dt.from_np(a.dtype), kind="ExternalInput").ap() for n, a in arrays.items()]
    out = nc.dram_tensor("out", (P, BLOCKS * FEAT), mybir.dt.float32, kind="ExternalOutput").ap()
    gnn_kernel(nc, *args, out)
    got = run_bass_kernel_spmd(nc, [arrays], core_ids=[0]).results[0]["out"]
    return np.ascontiguousarray(np.asarray(got).reshape(P, BLOCKS, FEAT).transpose(1, 0, 2)).reshape(NODES_PAD, FEAT)[:NODES]
```

```python
import numpy as np
import concourse.bass as bass
from concourse import mybir
from contextlib import ExitStack

P = 128
NODES, FEAT, HID, EDGE_F, TYPES = 12500, 64, 128, 32, 32
EDGES = 212500
TILES_PER_MACRO = 8
MACRO = P * TILES_PER_MACRO
MACROS = -(-EDGES // MACRO)
PAIRS = MACROS // 2
TILES = MACROS * TILES_PER_MACRO
EDGES_PAD = MACROS * MACRO
WINDOW = P - EDGE_F
CHUNK_BLOCKS, GROUP_BLOCKS = 9, 3
GROUPS = CHUNK_BLOCKS // GROUP_BLOCKS
BLOCKS = -(-(-(-(NODES + WINDOW) // P)) // CHUNK_BLOCKS) * CHUNK_BLOCKS
CHUNKS = BLOCKS // CHUNK_BLOCKS
NODES_PAD = BLOCKS * P
CHUNK_NODES = CHUNK_BLOCKS * P
CHUNK_COLS = CHUNK_BLOCKS * FEAT
GROUP_COLS = GROUP_BLOCKS * FEAT
PROJ = TYPES * FEAT
EPS = 1e-5
LAG = 8


def gnn_kernel(nc, x_in, src_in, type_in, norm_in, dst_in, dst_row, dst_first, due_in, edges_t, w_pre_in,
               w_edge_in, w2_in, b2_in, w_proj_in, bias_in, ident_in, window_row, window_col, out):
    f32, bf16, i32 = mybir.dt.float32, mybir.dt.bfloat16, mybir.dt.int32
    ALU, ACT, AX = mybir.AluOpType, mybir.ActivationFunctionType, mybir.AxisListType

    def table(name, shape, dt=f32):
        return nc.dram_tensor(name, shape, dt, kind="Internal").ap()

    p_table = table("p_table", [NODES_PAD, HID])
    q_table = table("q_table", [NODES_PAD, HID])
    proj_table = table("proj_table", [P + NODES_PAD, PROJ])
    proj_index = table("proj_index", [P, TILES], i32)
    window_place = table("window_place", [PAIRS, 2 * MACRO], bf16)
    p_rows = p_table.rearrange("(b p) f -> p b f", p=P)
    q_rows = q_table.rearrange("(b p) f -> p b f", p=P)
    proj_rows = proj_table.rearrange("(b p) f -> p b f", p=P)
    proj_by_type = proj_table.rearrange("n (r f) -> (n r) f", f=FEAT)
    place_row = window_place.rearrange("(a q) c -> a (q c)", a=1)

    keep = ExitStack()
    with keep:
        def buffer(where, name, shape, dt=f32):
            return where.enter_context(nc.sbuf_tensor(name, shape, dt))

        def bank(where, name, shape=(P, 512), dt=f32):
            return where.enter_context(nc.psum_tensor(name, list(shape), dt))

        def signal(where, name):
            return where.enter_context(nc.semaphore(name))

        x_sb = buffer(keep, "x_sb", [P, (1 + BLOCKS) * FEAT])
        acc = buffer(keep, "acc", [P, NODES_PAD])
        acc1 = buffer(keep, "acc1", [FEAT + 1, NODES_PAD])
        degree = acc1[FEAT:FEAT + 1, :]
        src_sb = buffer(keep, "src_sb", [P, TILES], i32)
        local_dst = buffer(keep, "local_dst", [P, TILES])
        first_sb = buffer(keep, "first_sb", [P, MACROS], i32)
        window_row_sb = buffer(keep, "window_row_sb", [P, WINDOW])
        window_col_sb = buffer(keep, "window_col_sb", [P, 1])
        ident = buffer(keep, "ident", [P, P])
        flag = buffer(keep, "flag", [1, 1], i32)

        with ExitStack() as s:
            centred = buffer(s, "centred", [P, CHUNK_COLS])
            squares = buffer(s, "squares", [P, CHUNK_COLS])
            stats = buffer(s, "stats", [P, 5, CHUNK_BLOCKS])
            h = buffer(s, "h", [P, CHUNK_COLS])
            h_t = buffer(s, "h_t", [FEAT + 1, GROUPS, GROUP_BLOCKS * P])
            w_pre = buffer(s, "w_pre", [FEAT + 1, 2 * HID + FEAT])
            staged = buffer(s, "staged", [P, GROUPS, GROUP_BLOCKS, 2 * HID])
            dst_sb = buffer(s, "dst_sb", [P, TILES], i32)
            type_sb = buffer(s, "type_sb", [P, TILES], i32)
            index_sb = buffer(s, "index_sb", [P, TILES], i32)
            dst_pairs = buffer(s, "dst_pairs", [PAIRS, 2, MACRO], i32)
            first_pairs = buffer(s, "first_pairs", [PAIRS, 2], i32)
            place = buffer(s, "place", [PAIRS, 2, MACRO])
            place_bf16 = buffer(s, "place_bf16", [PAIRS, 2, MACRO], bf16)
            broken = buffer(s, "broken", [P, 4])
            due = buffer(s, "due", [1, MACROS])
            late = buffer(s, "late", [1, MACROS])
            one_col = buffer(s, "one_col", [P, 1])
            ps_t = [bank(s, f"ps_t{g}") for g in range(2)]
            ps_pq = [bank(s, f"ps_pq{b}") for b in range(GROUP_BLOCKS)]
            ps_self = [bank(s, f"ps_self{g}") for g in range(2)]
            ps_flag = bank(s, "ps_flag")
            x_loaded, tables_loaded = signal(s, "x_loaded"), signal(s, "tables_loaded")
            step, var_ready, root_ready = signal(s, "step"), signal(s, "var_ready"), signal(s, "root_ready")
            h_ready, h_read = signal(s, "h_ready"), signal(s, "h_read")
            transposed, copied = signal(s, "transposed"), signal(s, "copied")
            pq_ready, pq_copied = signal(s, "pq_ready"), signal(s, "pq_copied")
            self_ready, self_added = signal(s, "self_ready"), signal(s, "self_added")
            staging_free = signal(s, "staging_free")
            index_step, indices_ready, places_ready = (signal(s, n) for n in ("index_step", "indices_ready", "places_ready"))
            broken_ready, flag_summed, tables_stored = (signal(s, n) for n in ("broken_ready", "flag_summed", "tables_stored"))
            turning = signal(s, "turning_0")
            ones_set, cleared = signal(s, "ones_set"), signal(s, "cleared")
            stored = [signal(s, f"stored{g}") for g in range(GROUPS)]
            block = s.enter_context(nc.Block())

            @block.sync
            def _(sp):
                sp.dma_start(x_sb[:, FEAT:], x_in).then_inc(x_loaded, 16)
                sp.dma_start(w_pre[:], w_pre_in).then_inc(x_loaded, 16)
                sp.dma_start(ident[:], ident_in).then_inc(x_loaded, 16)
                for to, of in ((src_sb[:], src_in), (type_sb[:], type_in), (dst_sb[:], dst_in),
                               (window_col_sb[:], window_col), (window_row_sb[:], window_row.partition_broadcast(P)[:, 0, :]),
                               (first_sb[:], dst_first.partition_broadcast(P)[:, 0, :]),
                               (dst_pairs[:].rearrange("q k c -> q (k c)"), dst_row.rearrange("a (q c) -> (a q) c", q=PAIRS)),
                               (first_pairs[:], dst_first.rearrange("a (q k) -> (a q) k", k=2)), (due[:], due_in)):
                    sp.dma_start(to, of).then_inc(tables_loaded, 16)
                sp.sem_inc(staging_free, GROUPS)
                with sp.Fori(0, CHUNKS) as c:
                    for g in range(GROUPS):
                        sp.wait_ge(pq_copied, c * CHUNK_BLOCKS + (g + 1) * GROUP_BLOCKS + GROUP_BLOCKS)
                        rows = bass.ds(c * CHUNK_BLOCKS + g * GROUP_BLOCKS, GROUP_BLOCKS)
                        sp.dma_start(p_rows[:, rows, :], staged[:, g, :, 0:HID]).then_inc(stored[g], 16)
                        sp.dma_start(q_rows[:, rows, :], staged[:, g, :, HID:2 * HID]).then_inc(stored[g], 16)
                        if g > 0:
                            sp.wait_ge(stored[g - 1], c * 32 + 32)
                            sp.sem_inc(staging_free, 1)
                    sp.wait_ge(stored[GROUPS - 1], c * 32 + 32)
                    sp.sem_inc(staging_free, 1)
                sp.wait_ge(indices_ready, 1)
                sp.dma_start(proj_index, index_sb[:]).then_inc(tables_stored, 16)
                sp.wait_ge(places_ready, 1)
                sp.dma_start(window_place, place_bf16[:].rearrange("q k c -> q (k c)")).then_inc(tables_stored, 16)
                sp.wait_ge(tables_stored, 32)

            @block.gpsimd
            def _(pool):
                pool.memset(acc[:], 0.0).then_inc(cleared, 1)
                pool.memset(acc1[:], 0.0).then_inc(cleared, 1)

            @block.vector
            def _(dve):
                dve.sem_inc(self_added, GROUPS)
                dve.sem_inc(h_read, 1)
                dve.memset(x_sb[:, 0:FEAT], 0.0).then_inc(cleared, 1)
                dve.memset(one_col[:], 1.0).then_inc(ones_set, 1)
                dve.memset(h_t[FEAT:FEAT + 1, :, :], 1.0).then_inc(ones_set, 1)
                dve.memset(broken[:], 0.0).then_inc(index_step, 1)
                dve.wait_ge(x_loaded, 48)
                steps = 7
                with dve.Fori(0, CHUNKS) as c:
                    xv = x_sb[:, bass.ds(c * CHUNK_COLS + FEAT, CHUNK_COLS)].rearrange("p (b f) -> p b f", f=FEAT)
                    cv = centred[:].rearrange("p (b f) -> p b f", f=FEAT)
                    sv = squares[:].rearrange("p (b f) -> p b f", f=FEAT)
                    wide = [P, CHUNK_BLOCKS, FEAT]
                    dve.tensor_reduce(stats[:, 0, :], xv, AX.X, ALU.add).then_inc(step, 1)
                    dve.wait_ge(step, c * steps + 1)
                    dve.tensor_scalar(stats[:, 1, :], stats[:, 0, :], -1.0 / FEAT, None, ALU.mult).then_inc(step, 1)
                    dve.wait_ge(step, c * steps + 2)
                    dve.tensor_tensor(cv, xv, stats[:, 1, :].unsqueeze(2).to_broadcast(wide), ALU.add).then_inc(step, 1)
                    dve.wait_ge(step, c * steps + 3)
                    dve.tensor_tensor(sv, cv, cv, ALU.mult).then_inc(step, 1)
                    dve.wait_ge(step, c * steps + 4)
                    dve.tensor_reduce(stats[:, 2, :], sv, AX.X, ALU.add).then_inc(step, 1)
                    dve.wait_ge(step, c * steps + 5)
                    dve.tensor_scalar(stats[:, 3, :], stats[:, 2, :], 1.0 / FEAT, EPS, ALU.mult, ALU.add).then_inc(var_ready, 1)
                    dve.wait_ge(root_ready, c + 1)
                    dve.reciprocal(stats[:, 4, :], stats[:, 3, :]).then_inc(step, 1)
                    dve.wait_ge(step, c * steps + 6)
                    dve.wait_ge(h_read, c + 1)
                    dve.scalar_tensor_tensor(h[:].rearrange("p (b f) -> p b f", f=FEAT), cv, 0.0,
                                             stats[:, 4, :].unsqueeze(2).to_broadcast(wide),
                                             ALU.max, ALU.mult).then_inc(h_ready, 1)
                    dve.wait_ge(h_ready, c + 1)
                    dve.tensor_copy(stats[:, 0, 0:1], stats[:, 0, 0:1]).then_inc(step, 1)
                    dve.wait_ge(step, c * steps + 7)
                    for g in range(GROUPS):
                        dve.wait_ge(self_ready, c * GROUPS + g + 1)
                        xg = x_sb[:, bass.ds(c * CHUNK_COLS + g * GROUP_COLS + FEAT, GROUP_COLS)]
                        dve.tensor_tensor(xg, xg, ps_self[g % 2][:, 0:GROUP_COLS], ALU.add).then_inc(self_added, 1)

                dve.wait_ge(tables_loaded, 9 * 16)
                dve.tensor_scalar(index_sb[:], src_sb[:], float(TYPES), float(P * TYPES), ALU.mult, ALU.add).then_inc(index_step, 1)
                dve.wait_ge(index_step, 2)
                dve.tensor_tensor(index_sb[:], index_sb[:], type_sb[:], ALU.add).then_inc(indices_ready, 1)
                per_tile = first_sb[:].unsqueeze(2).to_broadcast([P, MACROS, TILES_PER_MACRO])
                dve.tensor_tensor(local_dst[:].rearrange("p (m t) -> p m t", t=TILES_PER_MACRO),
                                  dst_sb[:].rearrange("p (m t) -> p m t", t=TILES_PER_MACRO), per_tile,
                                  ALU.subtract).then_inc(index_step, 1)
                for k in range(2):
                    dve.tensor_tensor(place[:, k, :], dst_pairs[:, k, :], first_pairs[:, k:k + 1].to_broadcast([PAIRS, MACRO]),
                                      ALU.subtract).then_inc(index_step, 1)
                dve.wait_ge(index_step, 5)
                dve.tensor_copy(place_bf16[:], place[:]).then_inc(places_ready, 1)
                outside = dst_pairs[:]
                for n, (bound, op) in enumerate(((0.0, ALU.is_lt), (WINDOW - 1.0, ALU.is_gt))):
                    dve.tensor_scalar(outside, place[:], bound, None, op).then_inc(index_step, 1)
                    dve.wait_ge(index_step, 6 + 2 * n)
                    dve.tensor_reduce(broken[0:PAIRS, n:n + 1], outside, AX.XY, ALU.add).then_inc(index_step, 1)
                    dve.wait_ge(index_step, 7 + 2 * n)
                dve.tensor_tensor(late[:], due[:], first_sb[0:1, :], ALU.is_gt).then_inc(index_step, 1)
                dve.wait_ge(index_step, 10)
                dve.tensor_reduce(broken[0:1, 2:3], late[:], AX.X, ALU.add).then_inc(index_step, 1)
                dve.wait_ge(index_step, 11)
                dve.tensor_reduce(broken[:, 3:4], broken[:, 0:3], AX.X, ALU.add).then_inc(broken_ready, 1)
                dve.wait_ge(flag_summed, 1)
                dve.tensor_copy(flag[:], ps_flag[0:1, 0:1]).then_inc(index_step, 1)

            @block.scalar
            def _(act):
                act.sem_inc(pq_copied, GROUP_BLOCKS)
                with act.Fori(0, CHUNKS) as c:
                    act.wait_ge(var_ready, c + 1)
                    act.activation(stats[:, 3, :], stats[:, 3, :], ACT.Sqrt).then_inc(root_ready, 1)

                    def copy_transposed(g):
                        act.wait_ge(transposed, c * GROUPS + g + 1)
                        act.activation(h_t[0:FEAT, g, :], ps_t[g % 2][0:FEAT, 0:GROUP_BLOCKS * P],
                                       ACT.Copy).then_inc(copied, 1)

                    def stage(g):
                        act.wait_ge(staging_free, c * GROUPS + g + 1)
                        for b in range(GROUP_BLOCKS):
                            act.wait_ge(pq_ready, c * CHUNK_BLOCKS + g * GROUP_BLOCKS + b + 1)
                            act.activation(staged[:, g, b, :], ps_pq[b][:, 0:2 * HID], ACT.Copy).then_inc(pq_copied, 1)

                    copy_transposed(0)
                    copy_transposed(1)
                    stage(0)
                    copy_transposed(2)
                    stage(1)
                    stage(2)

            @block.tensor
            def _(pe):
                pe.wait_ge(x_loaded, 48)
                pe.wait_ge(ones_set, 2)
                with pe.Fori(0, CHUNKS) as c:
                    pe.wait_ge(h_ready, c + 1)
                    pe.sem_inc(turning, 1)

                    def transpose(g):
                        for b in range(GROUP_BLOCKS):
                            col = (g * GROUP_BLOCKS + b) * FEAT
                            last = pe.transpose(ps_t[g % 2][0:FEAT, b * P:(b + 1) * P], h[:, col:col + FEAT], ident[:])
                        last.then_inc(transposed, 1)

                    def products(g):
                        pe.wait_ge(copied, c * GROUPS + g + 1)
                        for b in range(GROUP_BLOCKS):
                            pe.wait_ge(pq_copied, c * CHUNK_BLOCKS + g * GROUP_BLOCKS + b + 1)
                            pe.matmul(ps_pq[b][:, 0:2 * HID], h_t[:, g, b * P:(b + 1) * P], w_pre[:, 0:2 * HID],
                                      start=True, stop=True).then_inc(pq_ready, 1)
                        pe.wait_ge(self_added, c * GROUPS + (GROUPS, 2, 4)[g])
                        for b in range(GROUP_BLOCKS):
                            last = pe.matmul(ps_self[g % 2][:, b * FEAT:(b + 1) * FEAT], h_t[:, g, b * P:(b + 1) * P],
                                             w_pre[:, 2 * HID:], start=True, stop=True)
                        last.then_inc(self_ready, 1)

                    transpose(0)
                    transpose(1)
                    products(0)
                    transpose(2)
                    products(1)
                    pe.wait_ge(copied, c * GROUPS + GROUPS)
                    pe.sem_inc(h_read, 1)
                    products(2)
                pe.wait_ge(broken_ready, 1)
                pe.matmul(ps_flag[0:1, 0:1], broken[:, 3:4], one_col[:], start=True, stop=True).then_inc(flag_summed, 1)

        with ExitStack() as s:
            stack = buffer(s, "stack", [P, 2, MACRO])
            window_q = buffer(s, "window_q", [P, 2, HID])
            place_wide = buffer(s, "place_wide", [WINDOW, 2, MACRO], bf16)
            degree_part = buffer(s, "degree_part", [WINDOW, 2])
            one_hot = buffer(s, "one_hot", [P, 2, TILES_PER_MACRO, WINDOW])
            gathered = buffer(s, "gathered", [P, 2, 2, 4 * HID])
            index = buffer(s, "index", [P, 2, TILES_PER_MACRO], i32)
            edge_index = buffer(s, "edge_index", [P, 2], i32)
            edge_dst = buffer(s, "edge_dst", [1, P], i32)
            acc_now = buffer(s, "acc_now", [P, P])
            degree_now = buffer(s, "degree_now", [1, P])
            w2 = buffer(s, "w2", [HID, FEAT + 1])
            b2 = buffer(s, "b2", [1, FEAT + 1])
            bias = buffer(s, "bias", [P, FEAT])
            eps = buffer(s, "eps", [P, 1])
            x_now = buffer(s, "x_now", [P, FEAT])
            squares = buffer(s, "squares_0", [P, FEAT])
            normed = buffer(s, "normed", [P, FEAT])
            rest = buffer(s, "rest", [P, FEAT])
            stats = buffer(s, "stats_0", [P, 8])
            parts = buffer(s, "parts", [P, 3 * FEAT], bf16)
            parts_t = buffer(s, "parts_t", [P, 2, P], bf16)
            w_parts = buffer(s, "w_parts", [P, 3, PROJ + FEAT], bf16)
            ident_bf16 = buffer(s, "ident_bf16", [P, P], bf16)
            shared = buffer(s, "shared", [P, 2 * (PROJ + FEAT)])
            w_full, w_rest = shared[:, 0:PROJ + FEAT], shared[:, PROJ + FEAT:]
            staged = buffer(s, "staged_0", [P, PROJ])
            ps_pre = [bank(s, f"ps_pre{k}") for k in range(2)]
            ps_acc = [bank(s, f"ps_acc{k}") for k in range(2)]
            ps_proj = [bank(s, f"ps_proj{k}") for k in range(2)]
            ps_turn = bank(s, "ps_turn", (P, 1024), bf16)
            ps_block = bank(s, "ps_block")
            weights_loaded, split, consts_ready = signal(s, "weights_loaded"), signal(s, "split"), signal(s, "consts_ready")
            operands = [signal(s, f"operands{k}") for k in range(2)]
            places_loaded = [signal(s, f"places_loaded{k}") for k in range(2)]
            index_loaded = [signal(s, f"index_loaded{k}") for k in range(2)]
            landed = [[signal(s, f"landed{k}{f}") for f in range(2)] for k in range(2)]
            begun = signal(s, "begun")
            spread, hot_ready = signal(s, "spread"), signal(s, "hot_ready")
            pre_ready, summed, relu_done = signal(s, "pre_ready"), signal(s, "summed"), signal(s, "relu_done")
            half_used, sums_ready = signal(s, "half_used"), signal(s, "sums_ready")
            sums_added, degree_added = signal(s, "sums_added"), signal(s, "degree_added")
            acc_copied, degree_copied = signal(s, "acc_copied"), signal(s, "degree_copied")
            copying = signal(s, "copying")
            mean_ready, mean_read, link_step = signal(s, "mean_ready"), signal(s, "mean_read"), signal(s, "link_step")
            centre_ready, squared, root_ready = signal(s, "centre_ready"), signal(s, "squared"), signal(s, "root_ready")
            parts_ready, turned, turned_copied = signal(s, "parts_ready"), signal(s, "turned"), signal(s, "turned_copied")
            quarter_ready, quarter_copied = signal(s, "quarter_ready"), signal(s, "quarter_copied")
            self_ready, self_added = signal(s, "self_ready"), signal(s, "self_added")
            half_stored = [signal(s, f"half_stored{k}") for k in range(2)]
            tile_loaded, tile_gathered, tile_done = signal(s, "tile_loaded"), signal(s, "tile_gathered"), signal(s, "tile_done")
            tile_pre, tile_step, tile_turned = signal(s, "tile_pre"), signal(s, "tile_step"), signal(s, "tile_turned")
            loading = signal(s, "loading")
            adding = signal(s, "adding")
            tile_begun, edge_step = signal(s, "tile_begun"), signal(s, "edge_step")
            block = s.enter_context(nc.Block())
            HALVES = 4
            SPLITS = 6

            @block.sync
            def _(sp):
                for count, value in ((spread, 2), (half_used, HALVES), (pre_ready, HALVES), (summed, HALVES),
                                     (sums_added, 2), (tile_done, 1), (mean_read, 1), (quarter_copied, 2), (self_added, 1), (turned_copied, 1)):
                    sp.sem_inc(count, value)
                for k in range(2):
                    sp.dma_start(window_q[WINDOW:P, k, :], w_edge_in).then_inc(weights_loaded, 16)
                for k in range(2):
                    sp.dma_start(w_full[k * FEAT:(k + 1) * FEAT, :], w_proj_in).then_inc(weights_loaded, 16)
                for to, of in ((w2, w2_in), (b2, b2_in), (bias, bias_in.partition_broadcast(P)[:, 0, :])):
                    sp.dma_start(to[:], of).then_inc(weights_loaded, 16)
                broken_edges = sp.value_load(flag[0:1, 0:1], min_val=0, max_val=3 * EDGES_PAD)
                with sp.If(broken_edges == 0):
                    with sp.Fori(0, PAIRS) as i:
                        for k in range(2):
                            m = i * 2 + k
                            first = sp.value_load(first_sb[0:1, bass.ds(m, 1)], min_val=0, max_val=NODES)
                            sp.wait_ge(summed, m * 2 + 2)
                            sp.dma_start(index[:, k, :], src_sb[:, bass.ds(m * TILES_PER_MACRO, TILES_PER_MACRO)]
                                         ).then_inc(index_loaded[k], 16)
                            sp.wait_ge(spread, m + 1)
                            sp.dma_start(place_wide[:, k, :],
                                         place_row[0:1, bass.ds(m * MACRO, MACRO)].partition_broadcast(WINDOW)[:, 0, :]
                                         ).then_inc(places_loaded[k], 16)
                            sp.wait_ge(pre_ready, m * 2 + 2)
                            sp.sem_inc(loading, 1)
                            sp.dma_start(stack[WINDOW:P, k, :], edges_t[:, bass.ds(m * MACRO, MACRO)]).then_inc(operands[k], 16)
                            sp.dma_start(window_q[0:WINDOW, k, :], q_table[bass.ds(first, WINDOW), :]).then_inc(operands[k], 16)
                with sp.Else():
                    sp.wait_ge(weights_loaded, 7 * 16)
                    sp.dma_start(window_q[0:EDGE_F, 1, :], w_edge_in).then_inc(tile_loaded, 16)
                    with sp.Fori(0, TILES) as t:
                        sp.wait_ge(tile_done, t + 1)
                        sp.sem_inc(loading, 1)
                        sp.dma_start(edge_index[:, 0:1], src_in[:, bass.ds(t, 1)], allow_slow_non_contiguous=True).then_inc(tile_loaded, 16)
                        sp.dma_start(edge_index[:, 1:2], dst_in[:, bass.ds(t, 1)], allow_slow_non_contiguous=True).then_inc(tile_loaded, 16)
                        sp.dma_start(edge_dst[:], dst_row[0:1, bass.ds(t * P, P)]).then_inc(tile_loaded, 16)
                        sp.dma_start(stack[0:EDGE_F, 0, 0:P], edges_t[:, bass.ds(t * P, P)]).then_inc(tile_loaded, 16)

            @block.gpsimd
            def _(pool):
                broken_edges = pool.value_load(flag[0:1, 0:1], min_val=0, max_val=3 * EDGES_PAD)
                with pool.If(broken_edges == 0):
                    with pool.Fori(0, PAIRS) as i:
                        for k in range(2):
                            pool.wait_ge(index_loaded[k], i * 16 + 16)
                            for f in range(2):
                                pool.wait_ge(half_used, i * 4 + (k * 2 + f + 1))
                                pool.sem_inc(begun, 1)
                                for j in range(4):
                                    pool.indirect_dma_start(
                                        out=gathered[:, k, f, j * HID:(j + 1) * HID], out_offset=None, in_=p_table,
                                        in_offset=bass.IndirectOffsetOnAxis(ap=index[:, k, 4 * f + j:4 * f + j + 1], axis=0)
                                    ).then_inc(landed[k][f], 16)
                with pool.Else():
                    with pool.Fori(0, TILES) as t:
                        pool.wait_ge(tile_loaded, t * 64 + 80)
                        pool.sem_inc(tile_begun, 1)
                        for n, rows in enumerate((p_table, q_table)):
                            pool.indirect_dma_start(
                                out=gathered[:, 0, 0, n * HID:(n + 1) * HID], out_offset=None, in_=rows,
                                in_offset=bass.IndirectOffsetOnAxis(ap=edge_index[:, n:n + 1], axis=0)
                            ).then_inc(tile_gathered, 16)

            @block.vector
            def _(dve):
                dve.memset(eps[:], EPS).then_inc(consts_ready, 1)
                dve.memset(parts_t[:], 0.0).then_inc(consts_ready, 1)
                dve.tensor_copy(ident_bf16[:], ident[:]).then_inc(consts_ready, 1)
                dve.wait_ge(weights_loaded, 7 * 16)
                w1_part, w2_part, w3_part = (w_parts[:, n, :] for n in range(3))
                dve.tensor_copy(w1_part, w_full).then_inc(split, 1)
                dve.wait_ge(split, 1)
                dve.tensor_tensor(w_rest, w_full, w1_part, ALU.subtract).then_inc(split, 1)
                dve.wait_ge(split, 2)
                dve.tensor_copy(w2_part, w_rest).then_inc(split, 1)
                dve.wait_ge(split, 3)
                dve.tensor_tensor(w3_part[0:FEAT], w_rest[0:FEAT], w2_part[0:FEAT], ALU.subtract).then_inc(split, 1)
                dve.tensor_copy(w3_part[FEAT:P], w_full[FEAT:P]).then_inc(split, 1)
                dve.wait_ge(split, 5)
                dve.sem_inc(split, 1)

                LINKS = 6

                def mean_of(j):
                    n = j + 1
                    dve.wait_ge(mean_ready, n)
                    dve.tensor_scalar(stats[:, 0:1], ps_block[:, FEAT:FEAT + 1], 1.0, None, ALU.max).then_inc(link_step, 1)
                    dve.wait_ge(link_step, j * LINKS + 1)
                    dve.reciprocal(stats[:, 1:2], stats[:, 0:1]).then_inc(link_step, 1)
                    dve.wait_ge(link_step, j * LINKS + 2)
                    xj = x_sb[:, bass.ds(j * FEAT + FEAT, FEAT)]
                    dve.scalar_tensor_tensor(x_now[:], ps_block[:, 0:FEAT], stats[:, 1:2], xj, ALU.mult, ALU.add).then_inc(mean_read, 1)
                    dve.wait_ge(mean_read, j + 2)
                    dve.tensor_tensor(xj, x_now[:], bias[:], ALU.add).then_inc(link_step, 1)
                    dve.tensor_reduce(stats[:, 2:3], x_now[:], AX.X, ALU.add).then_inc(link_step, 1)
                    dve.wait_ge(link_step, j * LINKS + 4)
                    dve.tensor_scalar(stats[:, 3:4], stats[:, 2:3], -1.0 / FEAT, None, ALU.mult).then_inc(centre_ready, 1)

                def normalise(j):
                    dve.wait_ge(root_ready, j + 1)
                    dve.reciprocal(stats[:, 6:7], stats[:, 5:6]).then_inc(link_step, 1)
                    dve.wait_ge(link_step, j * LINKS + 5)
                    dve.tensor_scalar(normed[:], x_now[:], stats[:, 3:4], stats[:, 6:7], ALU.add, ALU.mult).then_inc(link_step, 1)
                    dve.wait_ge(link_step, j * LINKS + 6)
                    dve.tensor_scalar(parts[:, FEAT:2 * FEAT], normed[:], 0.0, None, ALU.max).then_inc(parts_ready, 1)
                    dve.wait_ge(parts_ready, j * 4 + 1)
                    dve.scalar_tensor_tensor(rest[:], normed[:], 0.0, parts[:, FEAT:2 * FEAT], ALU.max, ALU.subtract).then_inc(parts_ready, 1)
                    dve.wait_ge(parts_ready, j * 4 + 2)
                    dve.tensor_copy(parts[:, 0:FEAT], rest[:]).then_inc(parts_ready, 1)
                    dve.wait_ge(parts_ready, j * 4 + 3)
                    dve.tensor_tensor(parts[:, 2 * FEAT:], rest[:], parts[:, 0:FEAT], ALU.subtract).then_inc(parts_ready, 1)

                def add_self(j):
                    dve.wait_ge(self_ready, j + 1)
                    xj = x_sb[:, bass.ds(j * FEAT, FEAT)]
                    dve.tensor_tensor(xj, xj, ps_block[:, 128:128 + FEAT], ALU.add).then_inc(self_added, 1)

                def pair(i, with_block):
                    def spread_out(k):
                        m = i * 2 + k
                        dve.wait_ge(places_loaded[k], i * 16 + 16)
                        dve.wait_ge(pre_ready, m * 2 + 2)
                        dve.wait_ge(half_used, m * 2 + 2)
                        dve.tensor_scalar(stack[0:WINDOW, k, :], place_wide[:, k, :], window_col_sb[0:WINDOW, 0:1],
                                          None, ALU.is_equal, ALU.add, accum_out=degree_part[:, k:k + 1]).then_inc(spread, 1)
                        for t in range(TILES_PER_MACRO):
                            last = dve.tensor_scalar(one_hot[:, k, t, :], window_row_sb[:],
                                                     local_dst[:, bass.ds(m * TILES_PER_MACRO + t, 1)], None, ALU.is_equal)
                        last.then_inc(hot_ready, 1)

                    def add_gathered(k, f):
                        m = i * 2 + k
                        dve.wait_ge(pre_ready, m * 2 + (f + 1) + HALVES)
                        dve.wait_ge(landed[k][f], i * 64 + 64)
                        half = gathered[:, k, f, :]
                        dve.tensor_tensor(half, ps_pre[f][:], half, ALU.add).then_inc(summed, 1)

                    def accumulate(k):
                        m = i * 2 + k
                        first = dve.value_load(first_sb[0:1, bass.ds(m, 1)], min_val=0, max_val=NODES)
                        dve.wait_ge(sums_ready, m + 1)
                        dve.wait_ge(sums_added, m + 2)
                        to = degree[:, bass.ds(first, WINDOW)]
                        dve.tensor_tensor(to, to, ps_acc[k][0:1, 128:128 + WINDOW], ALU.add).then_inc(degree_added, 1)
                        dve.wait_ge(degree_added, m + 1)
                        to = acc[:, bass.ds(first, WINDOW)]
                        dve.tensor_tensor(to, to, ps_acc[k][:, 0:WINDOW], ALU.add).then_inc(sums_added, 1)

                    spread_out(0)
                    add_gathered(0, 0)
                    spread_out(1)
                    add_gathered(0, 1)
                    if with_block:
                        mean_of(i - LAG)
                    add_gathered(1, 0)
                    accumulate(0)
                    if with_block:
                        normalise(i - LAG)
                    add_gathered(1, 1)
                    accumulate(1)
                    if with_block:
                        add_self(i - LAG)

                def block_alone(j):
                    mean_of(j)
                    normalise(j)
                    add_self(j)

                broken_edges = dve.value_load(flag[0:1, 0:1], min_val=0, max_val=3 * EDGES_PAD)
                with dve.If(broken_edges == 0):
                    with dve.Fori(0, LAG) as i:
                        pair(i, False)
                    with dve.Fori(LAG, PAIRS) as i:
                        pair(i, True)
                    with dve.Fori(PAIRS - LAG, BLOCKS) as j:
                        block_alone(j)
                with dve.Else():
                    with dve.Fori(0, TILES) as t:
                        dve.wait_ge(tile_pre, t + 1)
                        dve.wait_ge(tile_gathered, t * 32 + 32)
                        mine, theirs = gathered[:, 0, 0, 0:HID], gathered[:, 0, 0, HID:2 * HID]
                        dve.tensor_tensor(mine, ps_pre[0][:, 0:HID], mine, ALU.add).then_inc(tile_step, 1)
                        dve.wait_ge(tile_step, t * 3 + 1)
                        dve.tensor_tensor(mine, mine, theirs, ALU.add).then_inc(tile_step, 1)
                        dve.wait_ge(tile_step, t * 3 + 2)
                        dve.tensor_scalar(mine, mine, 0.0, None, ALU.max).then_inc(tile_step, 1)
                        dve.wait_ge(tile_turned, t + 1)
                        dve.sem_inc(adding, 1)
                        with dve.Fori(0, P) as e:
                            node = dve.value_load(edge_dst[0:1, bass.ds(e, 1)], min_val=0, max_val=NODES)
                            to = degree[:, bass.ds(node, 1)]
                            dve.tensor_scalar(to, to, 1.0, None, ALU.add).then_inc(edge_step, 1)
                            to = acc[:, bass.ds(node, 1)]
                            dve.tensor_tensor(to, to, ps_acc[0][:, bass.ds(e, 1)], ALU.add).then_inc(edge_step, 1)
                            dve.wait_ge(edge_step, t * (2 * P) + e * 2 + 2)
                        dve.sem_inc(tile_done, 1)
                    dve.sem_inc(sums_added, 2 * PAIRS)
                    with dve.Fori(0, BLOCKS) as j:
                        block_alone(j)
                add_self(BLOCKS)

            @block.scalar
            def _(act):
                def copy_turned(j):
                    act.wait_ge(turned, j)
                    act.activation(parts_t[:].rearrange("p a c -> p (a c)"), ps_turn[:, 0:2 * P], ACT.Copy).then_inc(turned_copied, 1)

                def copy_quarter(j, q):
                    act.wait_ge(quarter_ready, j * 4 + (q + 1))
                    if q % 2 == 0:
                        act.wait_ge(half_stored[q // 2], j * 16 + 16)
                    act.activation(staged[:, q * 512:(q + 1) * 512], ps_proj[q % 2][:], ACT.Copy).then_inc(quarter_copied, 1)
                    if q % 2 == 1:
                        half = slice((q - 1) * 512, (q + 1) * 512)
                        act.wait_ge(quarter_copied, j * 4 + (q + 1) + 2)
                        act.dma_start(proj_rows[:, bass.ds(j, 1), half], staged[:, half].unsqueeze(1)
                                      ).then_inc(half_stored[q // 2], 16)

                def copy_sums(j):
                    act.activation(acc_now[:], acc[:, bass.ds(j * P, P)], ACT.Copy).then_inc(acc_copied, 1)
                    act.activation(degree_now[:], degree[:, bass.ds(j * P, P)], ACT.Copy).then_inc(degree_copied, 1)

                def root(j):
                    act.wait_ge(centre_ready, j + 1)
                    act.activation(squares[:], x_now[:], ACT.Square, bias=stats[:, 3:4], accum_out=stats[:, 4:5]).then_inc(squared, 1)
                    act.wait_ge(squared, j + 1)
                    act.activation(stats[:, 5:6], stats[:, 4:5], ACT.Sqrt, bias=eps[:], scale=1.0 / FEAT).then_inc(root_ready, 1)

                def relu(i, k, f):
                    act.wait_ge(summed, i * 4 + (k * 2 + f + 1) + HALVES)
                    half = gathered[:, k, f, :]
                    act.activation(half, half, ACT.Relu).then_inc(relu_done, 1)

                act.wait_ge(consts_ready, 3)
                act.wait_ge(split, SPLITS)
                act.activation(staged[:], w_rest[:, 0:PROJ], ACT.Copy, scale=0.0).then_inc(copying, 1)
                act.wait_ge(copying, 1)
                for half in range(2):
                    cols = slice(half * PROJ // 2, (half + 1) * PROJ // 2)
                    act.dma_start(proj_rows[:, 0:1, cols], staged[:, cols].unsqueeze(1)).then_inc(half_stored[half], 16)
                broken_edges = act.value_load(flag[0:1, 0:1], min_val=0, max_val=3 * EDGES_PAD)
                with act.If(broken_edges == 0):
                    with act.Fori(0, LAG) as i:
                        for k in range(2):
                            for f in range(2):
                                relu(i, k, f)
                    with act.Fori(LAG, PAIRS) as i:
                        j = i - LAG
                        relu(i, 0, 0)
                        copy_quarter(j, 0)
                        act.wait_ge(sums_added, i * 2 + 2)
                        act.sem_inc(copying, 1)
                        copy_sums(j)
                        relu(i, 0, 1)
                        copy_quarter(j, 1)
                        root(j)
                        relu(i, 1, 0)
                        copy_quarter(j, 2)
                        relu(i, 1, 1)
                        copy_quarter(j, 3)
                        copy_turned(j + 1)
                    act.wait_ge(sums_added, 2 * PAIRS + 2)
                    with act.Fori(PAIRS - LAG, BLOCKS) as j:
                        copy_quarter(j, 0)
                        copy_sums(j)
                        copy_quarter(j, 1)
                        root(j)
                        copy_quarter(j, 2)
                        copy_quarter(j, 3)
                        copy_turned(j + 1)
                with act.Else():
                    act.wait_ge(sums_added, 2 * PAIRS + 2)
                    with act.Fori(0, BLOCKS) as j:
                        copy_quarter(j, 0)
                        copy_sums(j)
                        copy_quarter(j, 1)
                        root(j)
                        copy_quarter(j, 2)
                        copy_quarter(j, 3)
                        copy_turned(j + 1)
                for q in range(4):
                    copy_quarter(BLOCKS, q)
                for half in range(2):
                    act.wait_ge(half_stored[half], (BLOCKS + 2) * 16)

            @block.tensor
            def _(pe):
                def project(to, cols):
                    for n, (left, right) in enumerate(((0, 1), (1, 2), (0, 0))):
                        last = pe.matmul(to, parts_t[:, left, :], w_parts[:, right, cols], start=(n == 0), stop=(n == 2))
                    return last

                def quarter(j, q):
                    if q == 0:
                        pe.wait_ge(turned_copied, j + 1)
                    pe.wait_ge(quarter_copied, j * 4 + (q + 1))
                    project(ps_proj[q % 2][:], slice(q * 512, (q + 1) * 512)).then_inc(quarter_ready, 1)

                def self_product(j):
                    pe.wait_ge(mean_read, j + 2)
                    project(ps_block[:, 128:128 + FEAT], slice(PROJ, PROJ + FEAT)).then_inc(self_ready, 1)

                def mean(j):
                    pe.wait_ge(acc_copied, j + 1)
                    pe.wait_ge(degree_copied, j + 1)
                    pe.wait_ge(self_added, j + 1)
                    pe.matmul(ps_block[:, 0:FEAT + 1], acc_now[:], w2[:], start=True, stop=False)
                    pe.matmul(ps_block[:, 0:FEAT + 1], degree_now[:], b2[:], start=False, stop=True).then_inc(mean_ready, 1)

                def turn(j):
                    pe.wait_ge(parts_ready, j * 4 + 4)
                    for n in range(2):
                        last = pe.transpose(ps_turn[:, n * P:(n + 1) * P], parts[:, n * FEAT:n * FEAT + P], ident_bf16[:])
                    last.then_inc(turned, 1)

                def pre(i, k, f):
                    m = i * 2 + k
                    if f == 0:
                        pe.wait_ge(operands[k], i * 32 + 32)
                        pe.wait_ge(spread, m + 3)
                    pe.wait_ge(summed, m * 2 + (f + 1) + 2)
                    for j in range(4):
                        col = (4 * f + j) * P
                        last = pe.matmul(ps_pre[f][:, j * HID:(j + 1) * HID], stack[:, k, col:col + P],
                                         window_q[:, k, :], start=True, stop=True)
                    last.then_inc(pre_ready, 1)

                def sums(i, k, f):
                    m = i * 2 + k
                    if f == 0:
                        pe.wait_ge(hot_ready, m + 1)
                        pe.wait_ge(sums_added, m + 1)
                        pe.matmul(ps_acc[k][:, 128:128 + WINDOW], degree_part[:, k:k + 1].to_broadcast([WINDOW, P]),
                                  ident[0:WINDOW, 0:WINDOW], start=True, stop=True)
                    pe.wait_ge(relu_done, m * 2 + (f + 1))
                    for j in range(4):
                        t = 4 * f + j
                        last = pe.matmul(ps_acc[k][:, 0:WINDOW], gathered[:, k, f, j * HID:(j + 1) * HID],
                                         one_hot[:, k, t, :], start=(t == 0), stop=(t == TILES_PER_MACRO - 1))
                    last.then_inc(half_used, 1)
                    if f == 1:
                        pe.wait_ge(half_used, m * 2 + 2 + HALVES)
                        pe.sem_inc(sums_ready, 1)

                def pair(i, with_block):
                    j = i - LAG
                    pre(i, 0, 0)
                    pre(i, 0, 1)
                    sums(i, 0, 0)
                    if with_block:
                        quarter(j, 0)
                    pre(i, 1, 0)
                    if with_block:
                        mean(j)
                    sums(i, 0, 1)
                    if with_block:
                        quarter(j, 1)
                    pre(i, 1, 1)
                    sums(i, 1, 0)
                    if with_block:
                        quarter(j, 2)
                    sums(i, 1, 1)
                    if with_block:
                        quarter(j, 3)
                        self_product(j)
                        turn(j)

                def block_alone(j):
                    quarter(j, 0)
                    mean(j)
                    quarter(j, 1)
                    quarter(j, 2)
                    quarter(j, 3)
                    self_product(j)
                    turn(j)

                pe.wait_ge(weights_loaded, 7 * 16)
                pe.wait_ge(consts_ready, 3)
                pe.wait_ge(split, SPLITS)
                broken_edges = pe.value_load(flag[0:1, 0:1], min_val=0, max_val=3 * EDGES_PAD)
                with pe.If(broken_edges == 0):
                    with pe.Fori(0, LAG) as i:
                        pair(i, False)
                    with pe.Fori(LAG, PAIRS) as i:
                        pair(i, True)
                    with pe.Fori(PAIRS - LAG, BLOCKS) as j:
                        block_alone(j)
                with pe.Else():
                    with pe.Fori(0, TILES) as t:
                        pe.wait_ge(tile_loaded, t * 64 + 80)
                        pe.matmul(ps_pre[0][:, 0:HID], stack[0:EDGE_F, 0, 0:P], window_q[0:EDGE_F, 1, :],
                                  start=True, stop=True).then_inc(tile_pre, 1)
                        pe.wait_ge(tile_step, t * 3 + 3)
                        pe.transpose(ps_acc[0][:, 0:P], gathered[:, 0, 0, 0:HID], ident[:]).then_inc(tile_turned, 1)
                    with pe.Fori(0, BLOCKS) as j:
                        block_alone(j)
                for q in range(4):
                    quarter(BLOCKS, q)
                pe.wait_ge(self_added, BLOCKS + 1)
                project(ps_block[:, 128:128 + FEAT], slice(PROJ, PROJ + FEAT)).then_inc(self_ready, 1)

        with ExitStack() as s:
            norm_sb = buffer(s, "norm_sb", [P, TILES])
            weighted = buffer(s, "weighted", [P, 2, TILES_PER_MACRO, WINDOW])
            messages = buffer(s, "messages", [P, 2, TILES_PER_MACRO, FEAT])
            index = buffer(s, "index_1", [P, 2, TILES_PER_MACRO], i32)
            edge_dst = buffer(s, "edge_dst_1", [1, P], i32)
            scaled = buffer(s, "scaled", [P, FEAT])
            ps_sum = [bank(s, f"ps_sum{k}") for k in range(2)]
            norm_loaded = signal(s, "norm_loaded")
            index_loaded = [signal(s, f"index_loaded_1{k}") for k in range(2)]
            landed = [signal(s, f"landed_1{k}") for k in range(2)]
            hot_ready, sums_ready, sums_added = signal(s, "hot_ready_1"), signal(s, "sums_ready_1"), signal(s, "sums_added_1")
            begun = signal(s, "begun_1")
            tile_loaded, tile_gathered, tile_done = (signal(s, n) for n in ("tile_loaded_1", "tile_gathered_1", "tile_done_1"))
            tile_scaled, tile_turned, edge_step = (signal(s, n) for n in ("tile_scaled", "tile_turned_1", "edge_step_1"))
            loading = signal(s, "loading_1")
            adding = signal(s, "adding_1")
            turning = signal(s, "turning")
            block = s.enter_context(nc.Block())

            @block.sync
            def _(sp):
                sp.sem_inc(sums_ready, 2)
                sp.sem_inc(sums_added, 2)
                sp.sem_inc(tile_done, 1)
                sp.dma_start(norm_sb[:], norm_in).then_inc(norm_loaded, 16)
                broken_edges = sp.value_load(flag[0:1, 0:1], min_val=0, max_val=3 * EDGES_PAD)
                with sp.If(broken_edges == 0):
                    with sp.Fori(0, PAIRS) as i:
                        for k in range(2):
                            m = i * 2 + k
                            sp.wait_ge(sums_ready, m + 1)
                            sp.dma_start(index[:, k, :], proj_index[:, bass.ds(m * TILES_PER_MACRO, TILES_PER_MACRO)]
                                         ).then_inc(index_loaded[k], 16)
                with sp.Else():
                    with sp.Fori(0, TILES) as t:
                        sp.wait_ge(tile_done, t + 1)
                        sp.sem_inc(loading, 1)
                        sp.dma_start(index[:, 0, 0:1], proj_index[:, bass.ds(t, 1)], allow_slow_non_contiguous=True).then_inc(tile_loaded, 16)
                        sp.dma_start(edge_dst[:], dst_row[0:1, bass.ds(t * P, P)]).then_inc(tile_loaded, 16)

            @block.gpsimd
            def _(pool):
                broken_edges = pool.value_load(flag[0:1, 0:1], min_val=0, max_val=3 * EDGES_PAD)
                with pool.If(broken_edges == 0):
                    with pool.Fori(0, PAIRS) as i:
                        for k in range(2):
                            pool.wait_ge(index_loaded[k], i * 16 + 16)
                            pool.sem_inc(begun, 1)
                            for t in range(TILES_PER_MACRO):
                                pool.indirect_dma_start(
                                    out=messages[:, k, t, :], out_offset=None, in_=proj_by_type,
                                    in_offset=bass.IndirectOffsetOnAxis(ap=index[:, k, t:t + 1], axis=0)
                                ).then_inc(landed[k], 16)
                with pool.Else():
                    with pool.Fori(0, TILES) as t:
                        pool.wait_ge(tile_loaded, t * 32 + 32)
                        pool.sem_inc(begun, 1)
                        pool.indirect_dma_start(
                            out=messages[:, 0, 0, :], out_offset=None, in_=proj_by_type,
                            in_offset=bass.IndirectOffsetOnAxis(ap=index[:, 0, 0:1], axis=0)
                        ).then_inc(tile_gathered, 16)

            @block.vector
            def _(dve):
                dve.wait_ge(norm_loaded, 16)
                broken_edges = dve.value_load(flag[0:1, 0:1], min_val=0, max_val=3 * EDGES_PAD)
                with dve.If(broken_edges == 0):
                    with dve.Fori(0, PAIRS) as i:
                        def weigh(k):
                            m = i * 2 + k
                            dve.wait_ge(sums_ready, m + 1)
                            for t in range(TILES_PER_MACRO):
                                tile = bass.ds(m * TILES_PER_MACRO + t, 1)
                                last = dve.tensor_scalar(weighted[:, k, t, :], window_row_sb[:], local_dst[:, tile],
                                                         norm_sb[:, tile], ALU.is_equal, ALU.mult)
                            last.then_inc(hot_ready, 1)

                        def accumulate(k):
                            m = i * 2 + k
                            first = dve.value_load(first_sb[0:1, bass.ds(m, 1)], min_val=0, max_val=NODES)
                            dve.wait_ge(sums_ready, m + 3)
                            dve.wait_ge(sums_added, m + 2)
                            to = acc1[0:FEAT, bass.ds(first, WINDOW)]
                            dve.tensor_tensor(to, to, ps_sum[k][0:FEAT, 0:WINDOW], ALU.add).then_inc(sums_added, 1)

                        weigh(0)
                        weigh(1)
                        accumulate(0)
                        accumulate(1)
                with dve.Else():
                    with dve.Fori(0, TILES) as t:
                        dve.wait_ge(tile_gathered, t * 16 + 16)
                        dve.tensor_scalar(scaled[:], messages[:, 0, 0, :], norm_sb[:, bass.ds(t, 1)], None, ALU.mult).then_inc(tile_scaled, 1)
                        dve.wait_ge(tile_turned, t + 1)
                        dve.sem_inc(adding, 1)
                        with dve.Fori(0, P) as e:
                            node = dve.value_load(edge_dst[0:1, bass.ds(e, 1)], min_val=0, max_val=NODES)
                            to = acc1[0:FEAT, bass.ds(node, 1)]
                            dve.tensor_tensor(to, to, ps_sum[0][0:FEAT, bass.ds(e, 1)], ALU.add).then_inc(edge_step, 1)
                            dve.wait_ge(edge_step, t * P + e + 1)
                        dve.sem_inc(tile_done, 1)

            @block.tensor
            def _(pe):
                broken_edges = pe.value_load(flag[0:1, 0:1], min_val=0, max_val=3 * EDGES_PAD)
                with pe.If(broken_edges == 0):
                    with pe.Fori(0, PAIRS) as i:
                        for k in range(2):
                            m = i * 2 + k
                            pe.wait_ge(hot_ready, m + 1)
                            pe.wait_ge(sums_added, m + 1)
                            pe.wait_ge(landed[k], i * 128 + 128)
                            for t in range(TILES_PER_MACRO):
                                last = pe.matmul(ps_sum[k][0:FEAT, 0:WINDOW], messages[:, k, t, :], weighted[:, k, t, :],
                                                 start=(t == 0), stop=(t == TILES_PER_MACRO - 1))
                            last.then_inc(sums_ready, 1)
                with pe.Else():
                    with pe.Fori(0, TILES) as t:
                        pe.wait_ge(tile_scaled, t + 1)
                        pe.sem_inc(turning, 1)
                        pe.transpose(ps_sum[0][0:FEAT, 0:P], scaled[:], ident[:]).then_inc(tile_turned, 1)

        with ExitStack() as s:
            acc_now = buffer(s, "acc1_now", [FEAT, 2, CHUNK_NODES])
            ps_out = [bank(s, f"ps_out{g}") for g in range(GROUPS)]
            chunk_copied, turned, added, stored = (signal(s, n) for n in ("chunk_copied", "turned_2", "added", "out_stored"))
            block = s.enter_context(nc.Block())

            @block.scalar
            def _(act):
                for c in range(CHUNKS):
                    if c >= 2:
                        act.wait_ge(turned, (c - 1) * GROUPS)
                    act.activation(acc_now[:, c % 2, :], acc1[0:FEAT, c * CHUNK_NODES:(c + 1) * CHUNK_NODES],
                                   ACT.Copy).then_inc(chunk_copied, 1)

            @block.tensor
            def _(pe):
                for c in range(CHUNKS):
                    pe.wait_ge(chunk_copied, c + 1)
                    for g in range(GROUPS):
                        if c > 0:
                            pe.wait_ge(added, (c - 1) * GROUPS + g + 1)
                        for b in range(GROUP_BLOCKS):
                            node = (g * GROUP_BLOCKS + b) * P
                            last = pe.transpose(ps_out[g][:, b * FEAT:(b + 1) * FEAT], acc_now[:, c % 2, node:node + P],
                                                ident[0:FEAT, 0:FEAT])
                        last.then_inc(turned, 1)

            @block.vector
            def _(dve):
                for n in range(CHUNKS * GROUPS):
                    dve.wait_ge(turned, n + 1)
                    xg = x_sb[:, FEAT + n * GROUP_COLS:FEAT + (n + 1) * GROUP_COLS]
                    dve.tensor_tensor(xg, xg, ps_out[n % GROUPS][:, 0:GROUP_COLS], ALU.add).then_inc(added, 1)

            @block.sync
            def _(sp):
                for c in range(CHUNKS):
                    sp.wait_ge(added, (c + 1) * GROUPS)
                    cols = slice(c * CHUNK_COLS, (c + 1) * CHUNK_COLS)
                    sp.dma_start(out[:, cols], x_sb[:, FEAT + c * CHUNK_COLS:FEAT + (c + 1) * CHUNK_COLS]).then_inc(stored, 16)
                sp.wait_ge(stored, 16 * CHUNKS)


def node_major(a):
    pad = np.zeros((NODES_PAD - NODES, FEAT), a.dtype)
    rows = np.concatenate([a, pad]).reshape(BLOCKS, P, FEAT)
    return np.ascontiguousarray(rows.transpose(1, 0, 2)).reshape(P, BLOCKS * FEAT)


def edge_major(a, pad):
    a = np.concatenate([a.reshape(-1), np.full(EDGES_PAD - EDGES, pad, a.dtype)])
    return np.ascontiguousarray(a.reshape(TILES, P).T)


def kernel(x, src, dst, edge_attr_32, edge_type_32, edge_weight1, L0_gnn_W1, L0_gnn_b1, L0_gnn_W2, L0_gnn_b2,
           L0_gnn_Wn, L0_gnn_bn, L1_gnn_W, L1_gnn_loop_weight, L1_gnn_h_bias):
    import concourse.bacc as bacc
    from concourse.bass_utils import run_bass_kernel_spmd

    (x, src, dst, edge_attr, edge_type, weight, w1, b1, w2, b2, wn, bn, w_rel, w_loop, bias) = (
        np.asarray(a) for a in (x, src, dst, edge_attr_32, edge_type_32, edge_weight1, L0_gnn_W1, L0_gnn_b1, L0_gnn_W2,
                                L0_gnn_b2, L0_gnn_Wn, L0_gnn_bn, L1_gnn_W, L1_gnn_loop_weight, L1_gnn_h_bias))
    f = np.float32
    dst_flat = np.concatenate([dst, np.full(EDGES_PAD - EDGES, NODES, dst.dtype)])
    w_pre = np.concatenate([np.concatenate([w1[0:FEAT], w1[FEAT:2 * FEAT], wn], axis=1),
                            np.concatenate([np.zeros(HID, f), b1, bn])[None, :]])
    w_rel = np.ascontiguousarray(w_rel.transpose(1, 0, 2)).reshape(FEAT, PROJ)
    due = np.maximum(P * (np.arange(MACROS) // 2 - LAG + 1), 0).astype(f)
    arrays = {
        "x_in": node_major(x),
        "src_in": edge_major(src, 0),
        "type_in": edge_major(edge_type, 0),
        "norm_in": edge_major(weight, 0),
        "dst_in": edge_major(dst, NODES),
        "dst_row": dst_flat[None, :],
        "dst_first": np.ascontiguousarray(dst_flat[::MACRO])[None, :],
        "due_in": due[None, :],
        "edges_t": np.ascontiguousarray(np.concatenate([edge_attr, np.zeros((EDGES_PAD - EDGES, EDGE_F), f)]).T),
        "w_pre_in": w_pre,
        "w_edge_in": np.ascontiguousarray(w1[2 * FEAT:]),
        "w2_in": np.concatenate([w2, np.zeros((HID, 1), f)], axis=1),
        "b2_in": np.concatenate([b2, np.ones(1, f)])[None, :],
        "w_proj_in": np.concatenate([w_rel, w_loop], axis=1),
        "bias_in": bias[None, :],
        "ident_in": np.eye(P, dtype=f),
        "window_row": np.arange(WINDOW, dtype=f)[None, :],
        "window_col": np.arange(P, dtype=f)[:, None],
    }
    nc = bacc.Bacc("TRN2", target_bir_lowering=False, num_devices=1)
    args = [nc.dram_tensor(n, a.shape, mybir.dt.from_np(a.dtype), kind="ExternalInput").ap() for n, a in arrays.items()]
    out = nc.dram_tensor("out", (P, BLOCKS * FEAT), mybir.dt.float32, kind="ExternalOutput").ap()
    gnn_kernel(nc, *args, out)
    got = run_bass_kernel_spmd(nc, [arrays], core_ids=[0]).results[0]["out"]
    return np.ascontiguousarray(np.asarray(got).reshape(P, BLOCKS, FEAT).transpose(1, 0, 2)).reshape(NODES_PAD, FEAT)[:NODES]
```

```python
import numpy as np
import concourse.bass as bass
from concourse import mybir
from contextlib import ExitStack

P = 128
NODES, FEAT, HID, EDGE_F, TYPES = 12500, 64, 128, 32, 32
EDGES = 212500
TILES_PER_MACRO = 8
MACRO = P * TILES_PER_MACRO
MACROS = -(-EDGES // MACRO)
PAIRS = MACROS // 2
TILES = MACROS * TILES_PER_MACRO
EDGES_PAD = MACROS * MACRO
WINDOW = P - EDGE_F
CHUNK_BLOCKS, GROUP_BLOCKS = 9, 3
GROUPS = CHUNK_BLOCKS // GROUP_BLOCKS
BLOCKS = -(-(-(-(NODES + WINDOW) // P)) // CHUNK_BLOCKS) * CHUNK_BLOCKS
CHUNKS = BLOCKS // CHUNK_BLOCKS
NODE_BLOCKS = -(-NODES // P)
NODES_PAD = BLOCKS * P
CHUNK_NODES = CHUNK_BLOCKS * P
CHUNK_COLS = CHUNK_BLOCKS * FEAT
GROUP_COLS = GROUP_BLOCKS * FEAT
PROJ = TYPES * FEAT
PRE = 2 * HID + FEAT
ROWS = 32
BIASES = 2 * HID + GROUP_COLS
EPS = 1e-5
TABLES_AT = CHUNKS // 3
LAG = 8
EARLY_EACH, EARLY_PAIRS = 2, 5
EARLY_CHUNKS = min(EARLY_EACH * EARLY_PAIRS, max(PAIRS - EARLY_PAIRS - LAG, 0) // CHUNK_BLOCKS)
TABLES_AT = CHUNKS // 3
LAG = 8
EARLY_CHUNKS = (PAIRS - LAG) // CHUNK_BLOCKS


def gnn_kernel(nc, x_in, src_in, type_in, norm_in, dst_in, dst_row, dst_first, due_in, edges_t, w_pre_in, bias_pre_in,
               w_edge_in, w2_in, b2_in, w_proj_in, bias_in, ident_in, window_row, window_col, out):
    f32, bf16, i32 = mybir.dt.float32, mybir.dt.bfloat16, mybir.dt.int32
    ALU, ACT, AX = mybir.AluOpType, mybir.ActivationFunctionType, mybir.AxisListType

    def table(name, shape, dt=f32):
        return nc.dram_tensor(name, shape, dt, kind="Internal").ap()

    p_table = table("p_table", [NODES_PAD, HID])
    q_table = table("q_table", [NODES_PAD, HID])
    proj_table = table("proj_table", [(1 + NODE_BLOCKS) * P, PROJ])
    proj_index = table("proj_index", [P, TILES], i32)
    window_place = table("window_place", [PAIRS, 2 * MACRO], bf16)
    p_rows = p_table.rearrange("(b p) f -> p b f", p=P)
    q_rows = q_table.rearrange("(b p) f -> p b f", p=P)
    proj_rows = proj_table.rearrange("(b p) f -> p b f", p=P)
    proj_by_type = proj_table.rearrange("n (r f) -> (n r) f", f=FEAT)
    place_row = window_place.rearrange("(a q) c -> a (q c)", a=1)

    keep = ExitStack()
    with keep:
        def buffer(where, name, shape, dt=f32):
            return where.enter_context(nc.sbuf_tensor(name, shape, dt))

        def bank(where, name, shape=(P, 512), dt=f32):
            return where.enter_context(nc.psum_tensor(name, list(shape), dt))

        def signal(where, name):
            return where.enter_context(nc.semaphore(name))

        x_sb = buffer(keep, "x_sb", [P, (1 + BLOCKS) * FEAT])
        acc = buffer(keep, "acc", [P, NODES_PAD])
        acc1 = buffer(keep, "acc1", [FEAT + 1, NODES_PAD])
        degree = acc1[FEAT:FEAT + 1, :]
        src_sb = buffer(keep, "src_sb", [P, TILES], i32)
        local_dst = buffer(keep, "local_dst", [P, TILES])
        first_sb = buffer(keep, "first_sb", [P, MACROS], i32)
        window_row_sb = buffer(keep, "window_row_sb", [P, WINDOW])
        window_col_sb = buffer(keep, "window_col_sb", [P, 1])
        ident = buffer(keep, "ident", [P, P])
        ident_bf16 = buffer(keep, "ident_bf16", [P, P], bf16)
        flag = buffer(keep, "flag", [1, 1], i32)
        first_index = buffer(keep, "first_index", [P, 2 * TILES_PER_MACRO], i32)
        window_q = buffer(keep, "window_q", [P, 2, HID])
        w2 = buffer(keep, "w2", [HID, FEAT + 1])
        b2 = buffer(keep, "b2", [1, FEAT + 1])
        bias = buffer(keep, "bias", [P, FEAT])
        w_parts = buffer(keep, "w_parts", [P, 3, PROJ + FEAT], bf16)

        with ExitStack() as s:
            centred = buffer(s, "centred", [P, CHUNK_COLS])
            squares = buffer(s, "squares", [P, CHUNK_COLS])
            stats = buffer(s, "stats", [P, 5, CHUNK_BLOCKS])
            h = buffer(s, "h", [P, CHUNK_COLS])
            h_parts = buffer(s, "h_parts", [P, CHUNK_BLOCKS, 3 * FEAT], bf16)
            h_parts_t = buffer(s, "h_parts_t", [P, GROUPS, 2 * GROUP_BLOCKS * P], bf16)
            w_pre_parts = buffer(s, "w_pre_parts", [P, 3, PRE], bf16)
            bias_parts = buffer(s, "bias_parts", [3 * ROWS, BIASES], bf16)
            add_rows = buffer(s, "add_rows", [3 * ROWS, P], bf16)
            staged = buffer(s, "staged", [P, GROUPS, GROUP_BLOCKS, 2 * HID])
            dst_sb = buffer(s, "dst_sb", [P, TILES], i32)
            type_sb = buffer(s, "type_sb", [P, TILES], i32)
            w_full, w_rest = acc[:, 0:PROJ + FEAT], acc[:, PROJ + FEAT:2 * (PROJ + FEAT)]
            later = 2 * (PROJ + FEAT) + TILES
            w_pre_full, w_pre_rest, bias_full, bias_rest = (acc[:, later + n * 512:later + n * 512 + cols]
                                                            for n, cols in enumerate((PRE, PRE, BIASES, BIASES)))
            bias_second = acc[:, later + 4 * 512:later + 5 * 512].bitcast(bf16)
            scaled_src = acc[:, 2 * (PROJ + FEAT):2 * (PROJ + FEAT) + TILES].bitcast(i32)
            dst_pairs = buffer(s, "dst_pairs", [PAIRS, 2, MACRO], i32)
            first_pairs = buffer(s, "first_pairs", [PAIRS, 2], i32)
            place_bf16 = buffer(s, "place_bf16", [PAIRS, 2, MACRO], bf16)
            broken = buffer(s, "broken", [P, 4])
            due = buffer(s, "due", [1, MACROS])
            late = buffer(s, "late", [1, MACROS])
            one_col = buffer(s, "one_col", [P, 1])
            beyond = buffer(s, "beyond", [P, 1])
            outside = acc[0:PAIRS, later + 5 * 512:later + 5 * 512 + MACRO].bitcast(bf16).rearrange("q (k c) -> q k c", k=2)
            ps_t = [bank(s, f"ps_t{g}", (P, 1024), bf16) for g in range(2)]
            ps_pq = [bank(s, f"ps_pq{b}") for b in range(GROUP_BLOCKS)]
            ps_self = [bank(s, f"ps_self{g}") for g in range(GROUPS)]
            ps_flag = ps_self[0]
            x_loaded, tables_loaded, weights_loaded = (signal(s, n) for n in ("x_loaded", "tables_loaded", "weights_loaded"))
            step, var_ready, root_ready = signal(s, "step"), signal(s, "var_ready"), signal(s, "root_ready")
            squares_ready = signal(s, "squares_ready")
            h_step, h_read, pre_split = signal(s, "h_step"), signal(s, "h_read"), signal(s, "pre_split")
            transposed, copied = signal(s, "transposed"), signal(s, "copied")
            pq_ready, pq_copied = signal(s, "pq_ready"), signal(s, "pq_copied")
            self_ready, self_added = signal(s, "self_ready"), signal(s, "self_added")
            staging_free = signal(s, "staging_free")
            index_step, indices_ready, places_ready = (signal(s, n) for n in ("index_step", "indices_ready", "places_ready"))
            index_scaled, places_done, outside_summed = (signal(s, n) for n in ("index_scaled", "places_done", "outside_summed"))
            x_first, split = signal(s, "x_first"), signal(s, "split")
            consts_loaded, ident_cast = signal(s, "consts_loaded"), signal(s, "ident_cast")
            broken_ready, flag_summed, tables_stored = (signal(s, n) for n in ("broken_ready", "flag_summed", "tables_stored"))
            turning = signal(s, "turning_0")
            ones_set, rows_set, cleared = signal(s, "ones_set"), signal(s, "rows_set"), signal(s, "cleared")
            stored = [signal(s, f"stored{g}") for g in range(GROUPS)]
            block = s.enter_context(nc.Block())
            STEPS, SPLITS, PRE_SPLITS = 5, 5, 10

            @block.sync
            def _(sp):
                sp.dma_start(x_sb[:, FEAT:FEAT + CHUNK_COLS], x_in[:, 0:CHUNK_COLS]).then_inc(x_first, 16)
                sp.dma_start(ident[:], ident_in).then_inc(consts_loaded, 16)
                for k in range(2):
                    sp.dma_start(w_pre_full[k * FEAT:(k + 1) * FEAT, :], w_pre_in[0:FEAT, :]).then_inc(consts_loaded, 16)
                sp.dma_start(bias_full, bias_pre_in.partition_broadcast(P)[:, 0, :]).then_inc(consts_loaded, 16)
                sp.dma_start(x_sb[:, FEAT + CHUNK_COLS:], x_in[:, CHUNK_COLS:]).then_inc(x_loaded, 16)
                for to, of in ((src_sb[:], src_in), (type_sb[:], type_in), (dst_sb[:], dst_in),
                               (window_col_sb[:], window_col), (window_row_sb[:], window_row.partition_broadcast(P)[:, 0, :]),
                               (first_sb[:], dst_first.partition_broadcast(P)[:, 0, :]),
                               (dst_pairs[:].rearrange("q k c -> q (k c)"), dst_row.rearrange("a (q c) -> (a q) c", q=PAIRS)),
                               (first_pairs[:], dst_first.rearrange("a (q k) -> (a q) k", k=2)), (due[:], due_in)):
                    sp.dma_start(to, of).then_inc(tables_loaded, 16)
                for k in range(2):
                    sp.dma_start(w_full[k * FEAT:(k + 1) * FEAT, :], w_proj_in).then_inc(weights_loaded, 16)
                    sp.dma_start(window_q[WINDOW:P, k, :], w_edge_in).then_inc(weights_loaded, 16)
                for to, of in ((w2, w2_in), (b2, b2_in), (bias, bias_in.partition_broadcast(P)[:, 0, :])):
                    sp.dma_start(to[:], of).then_inc(weights_loaded, 16)
                sp.sem_inc(staging_free, GROUPS)

                def store_chunk(c):
                    for g in range(GROUPS):
                        sp.wait_ge(pq_copied, c * CHUNK_BLOCKS + (g + 1) * GROUP_BLOCKS + GROUP_BLOCKS)
                        rows = bass.ds(c * CHUNK_BLOCKS + g * GROUP_BLOCKS, GROUP_BLOCKS)
                        sp.dma_start(p_rows[:, rows, :], staged[:, g, :, 0:HID]).then_inc(stored[g], 16)
                        sp.dma_start(q_rows[:, rows, :], staged[:, g, :, HID:2 * HID]).then_inc(stored[g], 16)
                        if g > 0:
                            sp.wait_ge(stored[g - 1], c * 32 + 32)
                            sp.sem_inc(staging_free, 1)
                    sp.wait_ge(stored[GROUPS - 1], c * 32 + 32)
                    sp.sem_inc(staging_free, 1)

                with sp.Fori(0, TABLES_AT + 3) as c:
                    store_chunk(c)
                sp.wait_ge(indices_ready, 1)
                sp.dma_start(proj_index, type_sb[:]).then_inc(tables_stored, 16)
                sp.wait_ge(places_ready, 1)
                sp.dma_start(window_place, place_bf16[:].rearrange("q k c -> q (k c)")).then_inc(tables_stored, 16)
                with sp.Fori(TABLES_AT + 3, CHUNKS) as c:
                    store_chunk(c)
                sp.wait_ge(tables_stored, 32)

            @block.gpsimd
            def _(pool):
                w1_part, w2_part, w3_part = (w_pre_parts[:, n, :] for n in range(3))
                pool.wait_ge(consts_loaded, 64)
                pool.tensor_copy(w1_part, w_pre_full).then_inc(pre_split, 1)
                pool.wait_ge(pre_split, 1)
                pool.tensor_tensor(w_pre_rest, w_pre_full, w1_part, ALU.subtract).then_inc(pre_split, 1)
                pool.wait_ge(pre_split, 2)
                pool.tensor_copy(w2_part, w_pre_rest).then_inc(pre_split, 1)
                pool.wait_ge(pre_split, 3)
                pool.tensor_copy(w3_part[FEAT:P], w_pre_full[FEAT:P]).then_inc(pre_split, 1)
                pool.wait_ge(pre_split, 4)
                pool.tensor_tensor(w3_part[0:FEAT], w_pre_rest[0:FEAT], w2_part[0:FEAT], ALU.subtract).then_inc(pre_split, 1)
                pool.wait_ge(pre_split, 5)
                pool.tensor_copy(bias_parts[:], bias_full[0:3 * ROWS]).then_inc(pre_split, 1)
                pool.wait_ge(pre_split, 6)
                pool.tensor_tensor(bias_rest[0:3 * ROWS], bias_full[0:3 * ROWS], bias_parts[:], ALU.subtract).then_inc(pre_split, 1)
                pool.wait_ge(pre_split, 7)
                pool.tensor_copy(bias_second[0:3 * ROWS, 0:BIASES], bias_rest[0:3 * ROWS]).then_inc(pre_split, 1)
                pool.wait_ge(pre_split, 8)
                pool.tensor_copy(bias_parts[ROWS:2 * ROWS], bias_second[ROWS:2 * ROWS, 0:BIASES]).then_inc(pre_split, 1)
                pool.wait_ge(pre_split, 9)
                pool.tensor_tensor(bias_parts[2 * ROWS:], bias_rest[2 * ROWS:3 * ROWS], bias_second[2 * ROWS:3 * ROWS, 0:BIASES],
                                   ALU.subtract).then_inc(pre_split, 1)
                pool.wait_ge(pre_split, PRE_SPLITS)
                pool.wait_ge(tables_loaded, 9 * 16)
                for k in range(2):
                    pool.tensor_tensor(dst_pairs[:, k, :], dst_pairs[:, k, :], first_pairs[:, k:k + 1].to_broadcast([PAIRS, MACRO]),
                                       ALU.subtract).then_inc(places_done, 1)
                per_tile = first_sb[:].unsqueeze(2).to_broadcast([P, MACROS, TILES_PER_MACRO])
                dst_by_macro = dst_sb[:].rearrange("p (m t) -> p m t", t=TILES_PER_MACRO)
                pool.tensor_tensor(dst_by_macro, dst_by_macro, per_tile, ALU.subtract).then_inc(places_done, 1)
                pool.tensor_scalar(type_sb[:], type_sb[:], float(P * TYPES), None, ALU.add).then_inc(index_scaled, 1)
                pool.tensor_scalar(scaled_src, src_sb[:], float(TYPES), None, ALU.mult).then_inc(index_scaled, 1)
                pool.wait_ge(index_scaled, 2)
                pool.tensor_tensor(type_sb[:], scaled_src, type_sb[:], ALU.add).then_inc(indices_ready, 1)
                pool.wait_ge(indices_ready, 1)
                pool.tensor_copy(first_index[:], type_sb[:, 0:2 * TILES_PER_MACRO]).then_inc(cleared, 1)
                w1_part, w2_part, w3_part = (w_parts[:, n, :] for n in range(3))
                pool.wait_ge(weights_loaded, 7 * 16)
                pool.tensor_copy(w1_part, w_full).then_inc(split, 1)
                pool.wait_ge(split, 1)
                pool.tensor_tensor(w_rest, w_full, w1_part, ALU.subtract).then_inc(split, 1)
                pool.wait_ge(split, 2)
                pool.tensor_copy(w2_part, w_rest).then_inc(split, 1)
                pool.wait_ge(split, 3)
                pool.tensor_tensor(w3_part[0:FEAT], w_rest[0:FEAT], w2_part[0:FEAT], ALU.subtract).then_inc(split, 1)
                pool.tensor_copy(w3_part[FEAT:P], w_full[FEAT:P]).then_inc(split, 1)
                pool.wait_ge(split, 5)
                pool.memset(acc1[:], 0.0).then_inc(cleared, 1)
                pool.wait_ge(outside_summed, 2)
                pool.memset(acc[:], 0.0).then_inc(cleared, 1)

            @block.vector
            def _(dve):
                dve.sem_inc(self_added, GROUPS)
                dve.sem_inc(h_read, 1)
                dve.memset(x_sb[:, 0:FEAT], 0.0).then_inc(cleared, 1)
                dve.memset(one_col[:], 1.0).then_inc(ones_set, 1)
                dve.memset(add_rows[:], 0.0).then_inc(rows_set, 1)
                dve.wait_ge(rows_set, 1)
                for n in range(3):
                    dve.memset(add_rows[n * ROWS:n * ROWS + 1, :], 1.0).then_inc(rows_set, 1)
                dve.memset(beyond[:], 1.0 - WINDOW).then_inc(ones_set, 1)
                dve.memset(broken[:], 0.0).then_inc(index_step, 1)
                steps = STEPS
                hv = h[:].rearrange("p (b f) -> p b f", f=FEAT)
                cv = centred[:].rearrange("p (b f) -> p b f", f=FEAT)
                sv = squares[:].rearrange("p (b f) -> p b f", f=FEAT)
                wide = [P, CHUNK_BLOCKS, FEAT]

                def normalise(c, between=None):
                    xv = x_sb[:, bass.ds(c * CHUNK_COLS + FEAT, CHUNK_COLS)].rearrange("p (b f) -> p b f", f=FEAT)
                    dve.tensor_reduce(stats[:, 0, :], xv, AX.X, ALU.add).then_inc(step, 1)
                    dve.wait_ge(step, c * steps + 1)
                    dve.tensor_scalar(stats[:, 1, :], stats[:, 0, :], -1.0 / FEAT, None, ALU.mult).then_inc(step, 1)
                    dve.wait_ge(step, c * steps + 2)
                    dve.tensor_tensor(cv, xv, stats[:, 1, :].unsqueeze(2).to_broadcast(wide), ALU.add).then_inc(step, 1)
                    if between:
                        between()
                    dve.wait_ge(squares_ready, c + 1)
                    dve.tensor_reduce(stats[:, 2, :], sv, AX.X, ALU.add).then_inc(step, 1)
                    dve.wait_ge(step, c * steps + 4)
                    dve.tensor_scalar(stats[:, 3, :], stats[:, 2, :], 1.0 / FEAT, EPS, ALU.mult, ALU.add).then_inc(var_ready, 1)
                    dve.wait_ge(root_ready, c + 1)
                    dve.reciprocal(stats[:, 4, :], stats[:, 3, :]).then_inc(step, 1)
                    dve.wait_ge(step, c * steps + 5)
                    dve.scalar_tensor_tensor(hv, cv, 0.0, stats[:, 4, :].unsqueeze(2).to_broadcast(wide),
                                             ALU.max, ALU.mult).then_inc(h_step, 1)
                    dve.wait_ge(h_read, c + 1)
                    dve.wait_ge(h_step, c * SPLITS + 1)
                    dve.tensor_copy(h_parts[:, :, FEAT:2 * FEAT], hv).then_inc(h_step, 1)
                    dve.wait_ge(h_step, c * SPLITS + 2)
                    dve.tensor_tensor(hv, hv, h_parts[:, :, FEAT:2 * FEAT], ALU.subtract).then_inc(h_step, 1)
                    dve.wait_ge(h_step, c * SPLITS + 3)
                    dve.tensor_copy(h_parts[:, :, 0:FEAT], hv).then_inc(h_step, 1)
                    dve.wait_ge(h_step, c * SPLITS + 4)
                    dve.tensor_tensor(h_parts[:, :, 2 * FEAT:], hv, h_parts[:, :, 0:FEAT], ALU.subtract).then_inc(h_step, 1)

                def add_self(c):
                    for g in range(GROUPS):
                        dve.wait_ge(self_ready, c * GROUPS + g + 1)
                        xg = x_sb[:, bass.ds(c * CHUNK_COLS + g * GROUP_COLS + FEAT, GROUP_COLS)]
                        dve.tensor_tensor(xg, xg, ps_self[g][:, 0:GROUP_COLS], ALU.add).then_inc(self_added, 1)

                dve.wait_ge(consts_loaded, 64)
                dve.tensor_copy(ident_bf16[:], ident[:]).then_inc(ident_cast, 1)
                dve.wait_ge(x_first, 16)
                normalise(0)
                dve.wait_ge(x_loaded, 16)

                def next_chunk(c, between=None):
                    dve.wait_ge(h_step, c * SPLITS + SPLITS)
                    normalise(c + 1, between)

                next_chunk(0)
                with dve.Fori(1, CHUNKS - 1) as c:
                    next_chunk(c, lambda: add_self(c - 1))
                add_self(CHUNKS - 2)
                add_self(CHUNKS - 1)

                dve.wait_ge(tables_loaded, 9 * 16)
                dve.tensor_tensor(late[:], due[:], first_sb[0:1, :], ALU.is_gt).then_inc(index_step, 1)
                dve.wait_ge(index_step, 2)
                dve.tensor_reduce(broken[0:1, 2:3], late[:], AX.X, ALU.add).then_inc(index_step, 1)
                dve.wait_ge(index_step, 3)
                dve.wait_ge(outside_summed, 2)
                dve.tensor_reduce(broken[:, 3:4], broken[:, 0:3], AX.X, ALU.add).then_inc(broken_ready, 1)
                dve.wait_ge(flag_summed, 1)
                dve.tensor_scalar(flag[:], ps_flag[0:1, 0:1], 1.0, None, ALU.min).then_inc(index_step, 1)

            @block.scalar
            def _(act):
                act.sem_inc(pq_copied, GROUP_BLOCKS)

                def square(c):
                    act.wait_ge(step, c * STEPS + 3)
                    act.activation(squares[:], centred[:], ACT.Square).then_inc(squares_ready, 1)

                def root(c):
                    act.wait_ge(var_ready, c + 1)
                    act.activation(stats[:, 3, :], stats[:, 3, :], ACT.Sqrt).then_inc(root_ready, 1)

                def chunk(c, last_chunk=False):
                    def copy_transposed(g):
                        act.wait_ge(transposed, c * GROUPS + g + 1)
                        act.activation(h_parts_t[:, g, :], ps_t[g % 2][:, 0:2 * GROUP_BLOCKS * P], ACT.Copy).then_inc(copied, 1)

                    def stage(g):
                        act.wait_ge(staging_free, c * GROUPS + g + 1)
                        for b in range(GROUP_BLOCKS):
                            act.wait_ge(pq_ready, c * CHUNK_BLOCKS + g * GROUP_BLOCKS + b + 1)
                            act.activation(staged[:, g, b, :], ps_pq[b][:, 0:2 * HID], ACT.Copy).then_inc(pq_copied, 1)

                    copy_transposed(0)
                    if not last_chunk:
                        square(c + 1)
                    copy_transposed(1)
                    stage(0)
                    if not last_chunk:
                        root(c + 1)
                    copy_transposed(2)
                    stage(1)
                    stage(2)

                square(0)
                root(0)
                with act.Fori(0, TABLES_AT) as c:
                    chunk(c)
                act.wait_ge(index_step, 1)
                act.wait_ge(places_done, 2)
                act.activation(place_bf16[:], dst_pairs[:], ACT.Copy).then_inc(places_ready, 1)
                chunk(TABLES_AT)
                act.activation(outside, dst_pairs[:], ACT.Relu, scale=-1.0, accum_out=broken[0:PAIRS, 0:1]).then_inc(outside_summed, 1)
                chunk(TABLES_AT + 1)
                act.wait_ge(outside_summed, 1)
                act.activation(outside, dst_pairs[:], ACT.Relu, bias=beyond[0:PAIRS], accum_out=broken[0:PAIRS, 1:2]).then_inc(outside_summed, 1)
                chunk(TABLES_AT + 2)
                act.wait_ge(places_done, 3)
                act.activation(local_dst[:], dst_sb[:], ACT.Copy).then_inc(cleared, 1)
                with act.Fori(TABLES_AT + 3, CHUNKS - 1) as c:
                    chunk(c)
                chunk(CHUNKS - 1, last_chunk=True)

            @block.tensor
            def _(pe):
                pe.wait_ge(ident_cast, 1)
                pe.wait_ge(pre_split, PRE_SPLITS)
                pe.wait_ge(rows_set, 4)
                with pe.Fori(0, CHUNKS) as c:
                    pe.wait_ge(h_step, c * SPLITS + SPLITS)
                    pe.sem_inc(turning, 1)

                    def transpose(g):
                        for b in range(GROUP_BLOCKS):
                            for n in range(2):
                                last = pe.transpose(ps_t[g % 2][:, (2 * b + n) * P:(2 * b + n + 1) * P],
                                                    h_parts[:, g * GROUP_BLOCKS + b, n * FEAT:n * FEAT + P], ident_bf16[:])
                        last.then_inc(transposed, 1)

                    def project(to, g, b, cols, last_in_bank):
                        for n, (left, right) in enumerate(((0, 1), (1, 2), (0, 0))):
                            at = (2 * b + left) * P
                            last = pe.matmul(to, h_parts_t[:, g, at:at + P], w_pre_parts[:, right, cols], start=False,
                                             stop=(n == 2 and last_in_bank))
                        return last

                    def products(g):
                        pe.wait_ge(copied, c * GROUPS + g + 1)
                        for b in range(GROUP_BLOCKS):
                            pe.wait_ge(pq_copied, c * CHUNK_BLOCKS + g * GROUP_BLOCKS + b + 1)
                            pe.matmul(ps_pq[b][:, 0:2 * HID], add_rows[:], bias_parts[:, 0:2 * HID], start=True, stop=False)
                            project(ps_pq[b][:, 0:2 * HID], g, b, slice(0, 2 * HID), True).then_inc(pq_ready, 1)
                        pe.wait_ge(self_added, c * GROUPS + g + 1)
                        pe.matmul(ps_self[g][:, 0:GROUP_COLS], add_rows[:], bias_parts[:, 2 * HID:], start=True, stop=False)
                        for b in range(GROUP_BLOCKS):
                            last = project(ps_self[g][:, b * FEAT:(b + 1) * FEAT], g, b, slice(2 * HID, PRE), b == GROUP_BLOCKS - 1)
                        last.then_inc(self_ready, 1)

                    transpose(0)
                    transpose(1)
                    products(0)
                    transpose(2)
                    products(1)
                    pe.wait_ge(copied, c * GROUPS + GROUPS)
                    pe.sem_inc(h_read, 1)
                    products(2)
                pe.wait_ge(broken_ready, 1)
                pe.matmul(ps_flag[0:1, 0:1], broken[:, 3:4], one_col[:], start=True, stop=True).then_inc(flag_summed, 1)

        with ExitStack() as s:
            stack = buffer(s, "stack", [P, 2, MACRO])
            place_wide = buffer(s, "place_wide", [WINDOW, 2, MACRO], bf16)
            degree_part = buffer(s, "degree_part", [WINDOW, 2])
            one_hot = buffer(s, "one_hot", [P, 2, TILES_PER_MACRO, WINDOW])
            gathered = buffer(s, "gathered", [P, 2, 2, 4 * HID])
            index = buffer(s, "index", [P, 2, TILES_PER_MACRO], i32)
            edge_index = buffer(s, "edge_index", [P, 2], i32)
            edge_dst = buffer(s, "edge_dst", [1, P], i32)
            acc_now = buffer(s, "acc_now", [P, P])
            degree_now = buffer(s, "degree_now", [1, P])
            eps = buffer(s, "eps", [P, 1])
            x_now = buffer(s, "x_now", [P, FEAT])
            squares = buffer(s, "squares_0", [P, FEAT])
            normed = buffer(s, "normed", [P, FEAT])
            rest = buffer(s, "rest", [P, FEAT])
            stats = buffer(s, "stats_0", [P, 8])
            parts = buffer(s, "parts", [P, 3 * FEAT], bf16)
            parts_t = buffer(s, "parts_t", [P, 2, P], bf16)
            staged = buffer(s, "staged_0", [P, PROJ])
            ps_pre = [bank(s, f"ps_pre{k}") for k in range(2)]
            ps_acc = [bank(s, f"ps_acc{k}") for k in range(2)]
            ps_proj = [bank(s, f"ps_proj{k}") for k in range(2)]
            ps_turn = bank(s, "ps_turn", (P, 1024), bf16)
            ps_block = bank(s, "ps_block")
            consts_ready = signal(s, "consts_ready")
            operands = [signal(s, f"operands{k}") for k in range(2)]
            places_loaded = [signal(s, f"places_loaded{k}") for k in range(2)]
            index_loaded = [signal(s, f"index_loaded{k}") for k in range(2)]
            landed = [[signal(s, f"landed{k}{f}") for f in range(2)] for k in range(2)]
            begun = signal(s, "begun")
            spread, hot_ready = signal(s, "spread"), signal(s, "hot_ready")
            pre_ready, summed, relu_done = signal(s, "pre_ready"), signal(s, "summed"), signal(s, "relu_done")
            half_used, sums_ready = signal(s, "half_used"), signal(s, "sums_ready")
            sums_added, degree_added = signal(s, "sums_added"), signal(s, "degree_added")
            acc_copied, degree_copied = signal(s, "acc_copied"), signal(s, "degree_copied")
            copying = signal(s, "copying")
            mean_ready, mean_read, link_step = signal(s, "mean_ready"), signal(s, "mean_read"), signal(s, "link_step")
            centre_ready, squared, root_ready = signal(s, "centre_ready"), signal(s, "squared"), signal(s, "root_ready")
            parts_ready, turned, turned_copied = signal(s, "parts_ready"), signal(s, "turned"), signal(s, "turned_copied")
            quarter_ready, quarter_copied = signal(s, "quarter_ready"), signal(s, "quarter_copied")
            self_ready, self_added = signal(s, "self_ready"), signal(s, "self_added")
            half_stored = [signal(s, f"half_stored{k}") for k in range(2)]
            tile_loaded, tile_gathered, tile_done = signal(s, "tile_loaded"), signal(s, "tile_gathered"), signal(s, "tile_done")
            tile_pre, tile_step, tile_turned = signal(s, "tile_pre"), signal(s, "tile_step"), signal(s, "tile_turned")
            loading = signal(s, "loading")
            adding = signal(s, "adding")
            tile_begun, edge_step = signal(s, "tile_begun"), signal(s, "edge_step")
            block = s.enter_context(nc.Block())
            HALVES = 4

            @block.sync
            def _(sp):
                for count, value in ((spread, 2), (half_used, HALVES), (pre_ready, HALVES), (summed, HALVES),
                                     (sums_added, 2), (tile_done, 1), (mean_read, 1), (quarter_copied, 2), (self_added, 1)):
                    sp.sem_inc(count, value)
                broken_edges = sp.value_load(flag[0:1, 0:1], min_val=0, max_val=1)
                with sp.If(broken_edges == 0):
                    def load_index(m, k):
                        sp.dma_start(index[:, k, :], src_sb[:, bass.ds(m * TILES_PER_MACRO, TILES_PER_MACRO)]
                                     ).then_inc(index_loaded[k], 16)

                    def load_pair(i, first_pair=False):
                        for k in range(2):
                            m = i * 2 + k
                            first = sp.value_load(first_sb[0:1, bass.ds(m, 1)], min_val=0, max_val=NODES)
                            sp.wait_ge(spread, m + 1)
                            sp.dma_start(place_wide[:, k, :],
                                         place_row[0:1, bass.ds(m * MACRO, MACRO)].partition_broadcast(WINDOW)[:, 0, :]
                                         ).then_inc(places_loaded[k], 16)
                            sp.wait_ge(pre_ready, m * 2 + 2)
                            sp.sem_inc(loading, 1)
                            sp.dma_start(stack[WINDOW:P, k, :], edges_t[:, bass.ds(m * MACRO, MACRO)]).then_inc(operands[k], 16)
                            sp.dma_start(window_q[0:WINDOW, k, :], q_table[bass.ds(first, WINDOW), :]).then_inc(operands[k], 16)
                            if not first_pair:
                                for f in range(2):
                                    sp.wait_ge(landed[k][f], i * 64)
                                load_index(m, k)

                    load_pair(0, first_pair=True)
                    with sp.Fori(1, PAIRS) as i:
                        load_pair(i)
                with sp.Else():
                    sp.dma_start(window_q[0:EDGE_F, 1, :], w_edge_in).then_inc(tile_loaded, 16)
                    with sp.Fori(0, TILES) as t:
                        sp.wait_ge(tile_done, t + 1)
                        sp.sem_inc(loading, 1)
                        sp.dma_start(edge_index[:, 0:1], src_in[:, bass.ds(t, 1)], allow_slow_non_contiguous=True).then_inc(tile_loaded, 16)
                        sp.dma_start(edge_index[:, 1:2], dst_in[:, bass.ds(t, 1)], allow_slow_non_contiguous=True).then_inc(tile_loaded, 16)
                        sp.dma_start(edge_dst[:], dst_row[0:1, bass.ds(t * P, P)]).then_inc(tile_loaded, 16)
                        sp.dma_start(stack[0:EDGE_F, 0, 0:P], edges_t[:, bass.ds(t * P, P)]).then_inc(tile_loaded, 16)

            @block.gpsimd
            def _(pool):
                broken_edges = pool.value_load(flag[0:1, 0:1], min_val=0, max_val=1)
                with pool.If(broken_edges == 0):
                    for k in range(2):
                        for f in range(2):
                            for j in range(4):
                                t = k * TILES_PER_MACRO + 4 * f + j
                                pool.indirect_dma_start(
                                    out=gathered[:, k, f, j * HID:(j + 1) * HID], out_offset=None, in_=p_table,
                                    in_offset=bass.IndirectOffsetOnAxis(ap=src_sb[:, t:t + 1], axis=0)
                                ).then_inc(landed[k][f], 16)
                    with pool.Fori(1, PAIRS) as i:
                        for k in range(2):
                            pool.wait_ge(index_loaded[k], i * 16)
                            for f in range(2):
                                pool.wait_ge(half_used, i * 4 + (k * 2 + f + 1))
                                pool.sem_inc(begun, 1)
                                for j in range(4):
                                    pool.indirect_dma_start(
                                        out=gathered[:, k, f, j * HID:(j + 1) * HID], out_offset=None, in_=p_table,
                                        in_offset=bass.IndirectOffsetOnAxis(ap=index[:, k, 4 * f + j:4 * f + j + 1], axis=0)
                                    ).then_inc(landed[k][f], 16)
                with pool.Else():
                    with pool.Fori(0, TILES) as t:
                        pool.wait_ge(tile_loaded, t * 64 + 80)
                        pool.sem_inc(tile_begun, 1)
                        for n, rows in enumerate((p_table, q_table)):
                            pool.indirect_dma_start(
                                out=gathered[:, 0, 0, n * HID:(n + 1) * HID], out_offset=None, in_=rows,
                                in_offset=bass.IndirectOffsetOnAxis(ap=edge_index[:, n:n + 1], axis=0)
                            ).then_inc(tile_gathered, 16)

            @block.vector
            def _(dve):
                dve.memset(eps[:], EPS).then_inc(consts_ready, 1)
                dve.memset(parts[:], 0.0).then_inc(consts_ready, 1)
                dve.memset(staged[:], 0.0).then_inc(consts_ready, 1)

                LINKS = 6

                def mean_of(j):
                    n = j + 1
                    dve.wait_ge(mean_ready, n)
                    dve.tensor_scalar(stats[:, 0:1], ps_block[:, FEAT:FEAT + 1], 1.0, None, ALU.max).then_inc(link_step, 1)
                    dve.wait_ge(link_step, j * LINKS + 1)
                    dve.reciprocal(stats[:, 1:2], stats[:, 0:1]).then_inc(link_step, 1)
                    dve.wait_ge(link_step, j * LINKS + 2)
                    xj = x_sb[:, bass.ds(j * FEAT + FEAT, FEAT)]
                    dve.scalar_tensor_tensor(x_now[:], ps_block[:, 0:FEAT], stats[:, 1:2], xj, ALU.mult, ALU.add).then_inc(mean_read, 1)
                    dve.wait_ge(mean_read, j + 2)
                    dve.tensor_tensor(xj, x_now[:], bias[:], ALU.add).then_inc(link_step, 1)
                    dve.tensor_reduce(stats[:, 2:3], x_now[:], AX.X, ALU.add).then_inc(link_step, 1)
                    dve.wait_ge(link_step, j * LINKS + 4)
                    dve.tensor_scalar(stats[:, 3:4], stats[:, 2:3], -1.0 / FEAT, None, ALU.mult).then_inc(centre_ready, 1)

                def normalise(j):
                    dve.wait_ge(root_ready, j + 1)
                    dve.reciprocal(stats[:, 6:7], stats[:, 5:6]).then_inc(link_step, 1)
                    dve.wait_ge(link_step, j * LINKS + 5)
                    dve.tensor_scalar(normed[:], x_now[:], stats[:, 3:4], stats[:, 6:7], ALU.add, ALU.mult).then_inc(link_step, 1)
                    dve.wait_ge(link_step, j * LINKS + 6)
                    dve.tensor_scalar(parts[:, FEAT:2 * FEAT], normed[:], 0.0, None, ALU.max).then_inc(parts_ready, 1)
                    dve.wait_ge(parts_ready, j * 4 + 1)
                    dve.scalar_tensor_tensor(rest[:], normed[:], 0.0, parts[:, FEAT:2 * FEAT], ALU.max, ALU.subtract).then_inc(parts_ready, 1)
                    dve.wait_ge(parts_ready, j * 4 + 2)
                    dve.tensor_copy(parts[:, 0:FEAT], rest[:]).then_inc(parts_ready, 1)
                    dve.wait_ge(parts_ready, j * 4 + 3)
                    dve.tensor_tensor(parts[:, 2 * FEAT:], rest[:], parts[:, 0:FEAT], ALU.subtract).then_inc(parts_ready, 1)

                def add_self(j):
                    dve.wait_ge(self_ready, j + 1)
                    xj = x_sb[:, bass.ds(j * FEAT, FEAT)]
                    dve.tensor_tensor(xj, xj, ps_block[:, 128:128 + FEAT], ALU.add).then_inc(self_added, 1)

                def spread_out(i, k):
                    m = i * 2 + k
                    dve.wait_ge(places_loaded[k], i * 16 + 16)
                    dve.wait_ge(pre_ready, m * 2 + 2)
                    dve.wait_ge(half_used, m * 2 + 2)
                    dve.tensor_scalar(stack[0:WINDOW, k, :], place_wide[:, k, :], window_col_sb[0:WINDOW, 0:1],
                                      None, ALU.is_equal, ALU.add, accum_out=degree_part[:, k:k + 1]).then_inc(spread, 1)
                    for t in range(TILES_PER_MACRO):
                        last = dve.tensor_scalar(one_hot[:, k, t, :], window_row_sb[:],
                                                 local_dst[:, bass.ds(m * TILES_PER_MACRO + t, 1)], None, ALU.is_equal)
                    last.then_inc(hot_ready, 1)

                def accumulate(i, k):
                    m = i * 2 + k
                    first = dve.value_load(first_sb[0:1, bass.ds(m, 1)], min_val=0, max_val=NODES)
                    dve.wait_ge(sums_ready, m + 1)
                    dve.wait_ge(sums_added, m + 2)
                    to = degree[:, bass.ds(first, WINDOW)]
                    dve.tensor_tensor(to, to, ps_acc[k][0:1, 128:128 + WINDOW], ALU.add).then_inc(degree_added, 1)
                    dve.wait_ge(degree_added, m + 1)
                    to = acc[:, bass.ds(first, WINDOW)]
                    dve.tensor_tensor(to, to, ps_acc[k][:, 0:WINDOW], ALU.add).then_inc(sums_added, 1)

                def pair(i, with_block, first_pair=False, first_block=False, last_pair=False):
                    def add_gathered(k, f):
                        m = i * 2 + k
                        dve.wait_ge(pre_ready, m * 2 + (f + 1) + HALVES)
                        dve.wait_ge(landed[k][f], i * 64 + 64)
                        half = gathered[:, k, f, :]
                        dve.tensor_tensor(half, ps_pre[f][:], half, ALU.add).then_inc(summed, 1)

                    add_gathered(0, 0)
                    if not first_pair:
                        accumulate(i - 1, 1)
                    if with_block and not first_block:
                        add_self(i - 1 - LAG)
                    spread_out(i, 1)
                    add_gathered(0, 1)
                    if with_block:
                        mean_of(i - LAG)
                    add_gathered(1, 0)
                    accumulate(i, 0)
                    if not last_pair:
                        spread_out(i + 1, 0)
                    if with_block:
                        normalise(i - LAG)
                    add_gathered(1, 1)

                def block_alone(j):
                    mean_of(j)
                    normalise(j)
                    add_self(j)

                broken_edges = dve.value_load(flag[0:1, 0:1], min_val=0, max_val=1)
                with dve.If(broken_edges == 0):
                    spread_out(0, 0)
                    pair(0, False, first_pair=True)
                    with dve.Fori(1, LAG) as i:
                        pair(i, False)
                    pair(LAG, True, first_block=True)
                    with dve.Fori(LAG + 1, PAIRS - 1) as i:
                        pair(i, True)
                    pair(PAIRS - 1, True, last_pair=True)
                    accumulate(PAIRS - 1, 1)
                    add_self(PAIRS - 1 - LAG)
                    with dve.Fori(PAIRS - LAG, NODE_BLOCKS) as j:
                        block_alone(j)
                with dve.Else():
                    with dve.Fori(0, TILES) as t:
                        dve.wait_ge(tile_pre, t + 1)
                        dve.wait_ge(tile_gathered, t * 32 + 32)
                        mine, theirs = gathered[:, 0, 0, 0:HID], gathered[:, 0, 0, HID:2 * HID]
                        dve.tensor_tensor(mine, ps_pre[0][:, 0:HID], mine, ALU.add).then_inc(tile_step, 1)
                        dve.wait_ge(tile_step, t * 3 + 1)
                        dve.tensor_tensor(mine, mine, theirs, ALU.add).then_inc(tile_step, 1)
                        dve.wait_ge(tile_step, t * 3 + 2)
                        dve.tensor_scalar(mine, mine, 0.0, None, ALU.max).then_inc(tile_step, 1)
                        dve.wait_ge(tile_turned, t + 1)
                        dve.sem_inc(adding, 1)
                        with dve.Fori(0, P) as e:
                            node = dve.value_load(edge_dst[0:1, bass.ds(e, 1)], min_val=0, max_val=NODES)
                            to = degree[:, bass.ds(node, 1)]
                            dve.tensor_scalar(to, to, 1.0, None, ALU.add).then_inc(edge_step, 1)
                            to = acc[:, bass.ds(node, 1)]
                            dve.tensor_tensor(to, to, ps_acc[0][:, bass.ds(e, 1)], ALU.add).then_inc(edge_step, 1)
                            dve.wait_ge(edge_step, t * (2 * P) + e * 2 + 2)
                        dve.sem_inc(tile_done, 1)
                    dve.sem_inc(sums_added, 2 * PAIRS)
                    with dve.Fori(0, NODE_BLOCKS) as j:
                        block_alone(j)
                add_self(NODE_BLOCKS)

            @block.scalar
            def _(act):
                def copy_turned(j):
                    act.wait_ge(turned, j + 1)
                    act.activation(parts_t[:].rearrange("p a c -> p (a c)"), ps_turn[:, 0:2 * P], ACT.Copy).then_inc(turned_copied, 1)

                def copy_quarter(j, q, staging=staged, fresh=False):
                    act.wait_ge(quarter_ready, j * 4 + (q + 1))
                    if q % 2 == 0 and not fresh:
                        act.wait_ge(half_stored[q // 2], j * 16 + 16)
                    act.activation(staging[:, q * 512:(q + 1) * 512], ps_proj[q % 2][:], ACT.Copy).then_inc(quarter_copied, 1)
                    if q % 2 == 1:
                        half = slice((q - 1) * 512, (q + 1) * 512)
                        act.wait_ge(quarter_copied, j * 4 + (q + 1) + 2)
                        act.dma_start(proj_rows[:, bass.ds(j, 1), half], staging[:, half].unsqueeze(1)
                                      ).then_inc(half_stored[q // 2], 16)

                def copy_sums(j):
                    act.activation(acc_now[:], acc[:, bass.ds(j * P, P)], ACT.Copy).then_inc(acc_copied, 1)
                    act.activation(degree_now[:], degree[:, bass.ds(j * P, P)], ACT.Copy).then_inc(degree_copied, 1)

                def root(j):
                    act.wait_ge(centre_ready, j + 1)
                    act.activation(squares[:], x_now[:], ACT.Square, bias=stats[:, 3:4], accum_out=stats[:, 4:5]).then_inc(squared, 1)
                    act.wait_ge(squared, j + 1)
                    act.activation(stats[:, 5:6], stats[:, 4:5], ACT.Sqrt, bias=eps[:], scale=1.0 / FEAT).then_inc(root_ready, 1)

                def relu(i, k, f):
                    act.wait_ge(summed, i * 4 + (k * 2 + f + 1) + HALVES)
                    half = gathered[:, k, f, :]
                    act.activation(half, half, ACT.Relu).then_inc(relu_done, 1)

                def block_alone(j):
                    copy_sums(j)
                    copy_turned(j)
                    copy_quarter(j, 0)
                    root(j)
                    for q in range(1, 4):
                        copy_quarter(j, q)

                act.wait_ge(consts_ready, 3)
                for half in range(2):
                    cols = slice(half * PROJ // 2, (half + 1) * PROJ // 2)
                    act.dma_start(proj_rows[:, 0:1, cols], staged[:, cols].unsqueeze(1)).then_inc(half_stored[half], 16)
                broken_edges = act.value_load(flag[0:1, 0:1], min_val=0, max_val=1)
                with act.If(broken_edges == 0):
                    with act.Fori(0, LAG) as i:
                        for k in range(2):
                            for f in range(2):
                                relu(i, k, f)
                    with act.Fori(LAG, PAIRS) as i:
                        j = i - LAG
                        relu(i, 0, 0)
                        copy_turned(j)
                        act.wait_ge(sums_added, i * 2 + 2)
                        act.sem_inc(copying, 1)
                        copy_sums(j)
                        copy_quarter(j, 0)
                        relu(i, 0, 1)
                        copy_quarter(j, 1)
                        root(j)
                        relu(i, 1, 0)
                        copy_quarter(j, 2)
                        relu(i, 1, 1)
                        copy_quarter(j, 3)
                    act.wait_ge(sums_added, 2 * PAIRS + 2)
                    with act.Fori(PAIRS - LAG, NODE_BLOCKS) as j:
                        block_alone(j)
                with act.Else():
                    act.wait_ge(sums_added, 2 * PAIRS + 2)
                    with act.Fori(0, NODE_BLOCKS) as j:
                        block_alone(j)
                copy_turned(NODE_BLOCKS)
                for q in range(4):
                    copy_quarter(NODE_BLOCKS, q, gathered[:].rearrange("p k f c -> p (k f c)"), fresh=True)
                for half in range(2):
                    act.wait_ge(half_stored[half], (NODE_BLOCKS + 2) * 16)

            @block.tensor
            def _(pe):
                def project(to, cols):
                    for n, (left, right) in enumerate(((0, 1), (1, 2), (0, 0))):
                        last = pe.matmul(to, parts_t[:, left, :], w_parts[:, right, cols], start=(n == 0), stop=(n == 2))
                    return last

                def quarter(j, q):
                    if q == 0:
                        pe.wait_ge(turned_copied, j + 1)
                    pe.wait_ge(quarter_copied, j * 4 + (q + 1))
                    project(ps_proj[q % 2][:], slice(q * 512, (q + 1) * 512)).then_inc(quarter_ready, 1)

                def self_product(j):
                    pe.wait_ge(mean_read, j + 2)
                    project(ps_block[:, 128:128 + FEAT], slice(PROJ, PROJ + FEAT)).then_inc(self_ready, 1)

                def mean(j):
                    pe.wait_ge(acc_copied, j + 1)
                    pe.wait_ge(degree_copied, j + 1)
                    pe.wait_ge(self_added, j + 1)
                    pe.matmul(ps_block[:, 0:FEAT + 1], acc_now[:], w2[:], start=True, stop=False)
                    pe.matmul(ps_block[:, 0:FEAT + 1], degree_now[:], b2[:], start=False, stop=True).then_inc(mean_ready, 1)

                def turn_parts():
                    for n in range(2):
                        last = pe.transpose(ps_turn[:, n * P:(n + 1) * P], parts[:, n * FEAT:n * FEAT + P], ident_bf16[:])
                    last.then_inc(turned, 1)

                def turn(j):
                    pe.wait_ge(parts_ready, j * 4 + 4)
                    turn_parts()

                def pre(i, k, f):
                    m = i * 2 + k
                    if f == 0:
                        pe.wait_ge(operands[k], i * 32 + 32)
                        pe.wait_ge(spread, m + 3)
                    pe.wait_ge(summed, m * 2 + (f + 1) + 2)
                    for j in range(4):
                        col = (4 * f + j) * P
                        last = pe.matmul(ps_pre[f][:, j * HID:(j + 1) * HID], stack[:, k, col:col + P],
                                         window_q[:, k, :], start=True, stop=True)
                    last.then_inc(pre_ready, 1)

                def sums(i, k, f):
                    m = i * 2 + k
                    if f == 0:
                        pe.wait_ge(hot_ready, m + 1)
                        pe.wait_ge(sums_added, m + 1)
                        pe.matmul(ps_acc[k][:, 128:128 + WINDOW], degree_part[:, k:k + 1].to_broadcast([WINDOW, P]),
                                  ident[0:WINDOW, 0:WINDOW], start=True, stop=True)
                    pe.wait_ge(relu_done, m * 2 + (f + 1))
                    for j in range(4):
                        t = 4 * f + j
                        last = pe.matmul(ps_acc[k][:, 0:WINDOW], gathered[:, k, f, j * HID:(j + 1) * HID],
                                         one_hot[:, k, t, :], start=(t == 0), stop=(t == TILES_PER_MACRO - 1))
                    last.then_inc(half_used, 1)
                    if f == 1:
                        pe.wait_ge(half_used, m * 2 + 2 + HALVES)
                        pe.sem_inc(sums_ready, 1)

                def pair(i, with_block, last_pair=False):
                    j = i - LAG
                    sums(i, 0, 0)
                    if with_block:
                        quarter(j, 0)
                        mean(j)
                    pre(i, 1, 0)
                    sums(i, 0, 1)
                    if with_block:
                        quarter(j, 1)
                    pre(i, 1, 1)
                    sums(i, 1, 0)
                    if with_block:
                        quarter(j, 2)
                    if not last_pair:
                        pre(i + 1, 0, 0)
                    sums(i, 1, 1)
                    if with_block:
                        quarter(j, 3)
                        self_product(j)
                    if not last_pair:
                        pre(i + 1, 0, 1)
                    if with_block:
                        turn(j)

                def block_alone(j):
                    mean(j)
                    for q in range(4):
                        quarter(j, q)
                    self_product(j)
                    turn(j)

                pe.wait_ge(consts_ready, 2)
                turn_parts()
                broken_edges = pe.value_load(flag[0:1, 0:1], min_val=0, max_val=1)
                with pe.If(broken_edges == 0):
                    pre(0, 0, 0)
                    pre(0, 0, 1)
                    with pe.Fori(0, LAG) as i:
                        pair(i, False)
                    with pe.Fori(LAG, PAIRS - 1) as i:
                        pair(i, True)
                    pair(PAIRS - 1, True, last_pair=True)
                    with pe.Fori(PAIRS - LAG, NODE_BLOCKS) as j:
                        block_alone(j)
                with pe.Else():
                    with pe.Fori(0, TILES) as t:
                        pe.wait_ge(tile_loaded, t * 64 + 80)
                        pe.matmul(ps_pre[0][:, 0:HID], stack[0:EDGE_F, 0, 0:P], window_q[0:EDGE_F, 1, :],
                                  start=True, stop=True).then_inc(tile_pre, 1)
                        pe.wait_ge(tile_step, t * 3 + 3)
                        pe.transpose(ps_acc[0][:, 0:P], gathered[:, 0, 0, 0:HID], ident[:]).then_inc(tile_turned, 1)
                    with pe.Fori(0, NODE_BLOCKS) as j:
                        block_alone(j)
                for q in range(4):
                    quarter(NODE_BLOCKS, q)
                pe.wait_ge(self_added, NODE_BLOCKS + 1)
                project(ps_block[:, 128:128 + FEAT], slice(PROJ, PROJ + FEAT)).then_inc(self_ready, 1)

        def finishing(where, name, first=0):
            banks = [bank(where, f"ps_out{g}_{name}") for g in range(GROUPS)]
            turned, added, stored = (signal(where, f"{what}_{name}") for what in ("out_turned", "out_added", "out_stored"))

            def turn(pe, chunks):
                for c in chunks:
                    for g in range(GROUPS):
                        if c > first:
                            pe.wait_ge(added, (c - first - 1) * GROUPS + g + 1)
                        for b in range(GROUP_BLOCKS):
                            node = (c * CHUNK_BLOCKS + g * GROUP_BLOCKS + b) * P
                            last = pe.transpose(banks[g][:, b * FEAT:(b + 1) * FEAT], acc1[0:FEAT, node:node + P],
                                                ident[0:FEAT, 0:FEAT])
                        last.then_inc(turned, 1)

            def add(dve, chunks):
                for c in chunks:
                    for g in range(GROUPS):
                        dve.wait_ge(turned, (c - first) * GROUPS + g + 1)
                        at = FEAT + c * CHUNK_COLS + g * GROUP_COLS
                        xg = x_sb[:, at:at + GROUP_COLS]
                        dve.tensor_tensor(xg, xg, banks[g][:, 0:GROUP_COLS], ALU.add).then_inc(added, 1)

            def store(sp, chunks):
                for c in chunks:
                    sp.wait_ge(added, (c - first + 1) * GROUPS)
                    sp.dma_start(out[:, c * CHUNK_COLS:(c + 1) * CHUNK_COLS],
                                 x_sb[:, FEAT + c * CHUNK_COLS:FEAT + (c + 1) * CHUNK_COLS]).then_inc(stored, 16)
                sp.wait_ge(stored, 16 * len(chunks))

            return turn, add, store

        early, late_chunks = range(EARLY_CHUNKS), range(EARLY_CHUNKS, CHUNKS)
        early_of_pair = [early[n * EARLY_EACH:(n + 1) * EARLY_EACH] for n in range(EARLY_PAIRS)]

        with ExitStack() as s:
            norm_sb = buffer(s, "norm_sb", [P, TILES])
            weighted = buffer(s, "weighted", [P, 2, TILES_PER_MACRO, WINDOW])
            messages = buffer(s, "messages", [P, 2, TILES_PER_MACRO, FEAT])
            index = buffer(s, "index_1", [P, 2, TILES_PER_MACRO], i32)
            edge_dst = buffer(s, "edge_dst_1", [1, P], i32)
            scaled = buffer(s, "scaled", [P, FEAT])
            ps_sum = [bank(s, f"ps_sum{k}") for k in range(2)]
            turn_early, add_early, store_early = finishing(s, "early")
            norm_loaded = signal(s, "norm_loaded")
            index_loaded = [signal(s, f"index_loaded_1{k}") for k in range(2)]
            landed = [signal(s, f"landed_1{k}") for k in range(2)]
            hot_ready, sums_ready, sums_added = signal(s, "hot_ready_1"), signal(s, "sums_ready_1"), signal(s, "sums_added_1")
            begun = signal(s, "begun_1")
            tile_loaded, tile_gathered, tile_done = (signal(s, n) for n in ("tile_loaded_1", "tile_gathered_1", "tile_done_1"))
            tile_scaled, tile_turned, edge_step = (signal(s, n) for n in ("tile_scaled", "tile_turned_1", "edge_step_1"))
            loading = signal(s, "loading_1")
            adding = signal(s, "adding_1")
            turning = signal(s, "turning")
            block = s.enter_context(nc.Block())

            @block.sync
            def _(sp):
                sp.sem_inc(sums_ready, 2)
                sp.sem_inc(sums_added, 2)
                sp.sem_inc(tile_done, 1)
                sp.dma_start(norm_sb[:], norm_in).then_inc(norm_loaded, 16)
                broken_edges = sp.value_load(flag[0:1, 0:1], min_val=0, max_val=1)
                with sp.If(broken_edges == 0):
                    with sp.Fori(1, PAIRS) as i:
                        for k in range(2):
                            m = i * 2 + k
                            sp.wait_ge(sums_ready, m + 1)
                            sp.dma_start(index[:, k, :], proj_index[:, bass.ds(m * TILES_PER_MACRO, TILES_PER_MACRO)]
                                         ).then_inc(index_loaded[k], 16)
                    store_early(sp, early)
                with sp.Else():
                    with sp.Fori(0, TILES) as t:
                        sp.wait_ge(tile_done, t + 1)
                        sp.sem_inc(loading, 1)
                        sp.dma_start(index[:, 0, 0:1], proj_index[:, bass.ds(t, 1)], allow_slow_non_contiguous=True).then_inc(tile_loaded, 16)
                        sp.dma_start(edge_dst[:], dst_row[0:1, bass.ds(t * P, P)]).then_inc(tile_loaded, 16)

            @block.gpsimd
            def _(pool):
                broken_edges = pool.value_load(flag[0:1, 0:1], min_val=0, max_val=1)
                with pool.If(broken_edges == 0):
                    def gather(k, indices):
                        for t in range(TILES_PER_MACRO):
                            pool.indirect_dma_start(
                                out=messages[:, k, t, :], out_offset=None, in_=proj_by_type,
                                in_offset=bass.IndirectOffsetOnAxis(ap=indices[:, t:t + 1], axis=0)
                            ).then_inc(landed[k], 16)

                    for k in range(2):
                        gather(k, first_index[:, k * TILES_PER_MACRO:(k + 1) * TILES_PER_MACRO])
                    with pool.Fori(1, PAIRS) as i:
                        for k in range(2):
                            pool.wait_ge(index_loaded[k], i * 16)
                            pool.sem_inc(begun, 1)
                            gather(k, index[:, k, :])
                with pool.Else():
                    with pool.Fori(0, TILES) as t:
                        pool.wait_ge(tile_loaded, t * 32 + 32)
                        pool.sem_inc(begun, 1)
                        pool.indirect_dma_start(
                            out=messages[:, 0, 0, :], out_offset=None, in_=proj_by_type,
                            in_offset=bass.IndirectOffsetOnAxis(ap=index[:, 0, 0:1], axis=0)
                        ).then_inc(tile_gathered, 16)

            @block.vector
            def _(dve):
                dve.wait_ge(norm_loaded, 16)
                broken_edges = dve.value_load(flag[0:1, 0:1], min_val=0, max_val=1)
                with dve.If(broken_edges == 0):
                    def weigh(m, k):
                        dve.wait_ge(sums_ready, m + 1)
                        for t in range(TILES_PER_MACRO):
                            tile = bass.ds(m * TILES_PER_MACRO + t, 1)
                            last = dve.tensor_scalar(weighted[:, k, t, :], window_row_sb[:], local_dst[:, tile],
                                                     norm_sb[:, tile], ALU.is_equal, ALU.mult)
                        last.then_inc(hot_ready, 1)

                    def accumulate(m, k):
                        first = dve.value_load(first_sb[0:1, bass.ds(m, 1)], min_val=0, max_val=NODES)
                        dve.wait_ge(sums_ready, m + 3)
                        dve.wait_ge(sums_added, m + 2)
                        to = acc1[0:FEAT, bass.ds(first, WINDOW)]
                        dve.tensor_tensor(to, to, ps_sum[k][0:FEAT, 0:WINDOW], ALU.add).then_inc(sums_added, 1)

                    def pair(i, chunks=()):
                        weigh(i * 2, 0)
                        weigh(i * 2 + 1, 1)
                        add_early(dve, chunks)
                        accumulate(i * 2, 0)
                        accumulate(i * 2 + 1, 1)

                    with dve.Fori(0, PAIRS - EARLY_PAIRS) as i:
                        pair(i)
                    for n, chunks in enumerate(early_of_pair):
                        pair(PAIRS - EARLY_PAIRS + n, chunks)
                with dve.Else():
                    with dve.Fori(0, TILES) as t:
                        dve.wait_ge(tile_gathered, t * 16 + 16)
                        dve.tensor_scalar(scaled[:], messages[:, 0, 0, :], norm_sb[:, bass.ds(t, 1)], None, ALU.mult).then_inc(tile_scaled, 1)
                        dve.wait_ge(tile_turned, t + 1)
                        dve.sem_inc(adding, 1)
                        with dve.Fori(0, P) as e:
                            node = dve.value_load(edge_dst[0:1, bass.ds(e, 1)], min_val=0, max_val=NODES)
                            to = acc1[0:FEAT, bass.ds(node, 1)]
                            dve.tensor_tensor(to, to, ps_sum[0][0:FEAT, bass.ds(e, 1)], ALU.add).then_inc(edge_step, 1)
                            dve.wait_ge(edge_step, t * P + e + 1)
                        dve.sem_inc(tile_done, 1)

            @block.tensor
            def _(pe):
                broken_edges = pe.value_load(flag[0:1, 0:1], min_val=0, max_val=1)
                with pe.If(broken_edges == 0):
                    def sums(m, k, macros_landed):
                        pe.wait_ge(hot_ready, m + 1)
                        pe.wait_ge(sums_added, m + 1)
                        pe.wait_ge(landed[k], macros_landed * 128)
                        for t in range(TILES_PER_MACRO):
                            last = pe.matmul(ps_sum[k][0:FEAT, 0:WINDOW], messages[:, k, t, :], weighted[:, k, t, :],
                                             start=(t == 0), stop=(t == TILES_PER_MACRO - 1))
                        last.then_inc(sums_ready, 1)

                    with pe.Fori(0, PAIRS - EARLY_PAIRS) as i:
                        for k in range(2):
                            sums(i * 2 + k, k, i + 1)
                    for n, chunks in enumerate(early_of_pair):
                        i = PAIRS - EARLY_PAIRS + n
                        pe.wait_ge(sums_added, i * 2 + 2)
                        turn_early(pe, chunks)
                        for k in range(2):
                            sums(i * 2 + k, k, i + 1)
                with pe.Else():
                    with pe.Fori(0, TILES) as t:
                        pe.wait_ge(tile_scaled, t + 1)
                        pe.sem_inc(turning, 1)
                        pe.transpose(ps_sum[0][0:FEAT, 0:P], scaled[:], ident[:]).then_inc(tile_turned, 1)

        with ExitStack() as s:
            turn_late, add_late, store_late = finishing(s, "late", EARLY_CHUNKS)
            turn_all, add_all, store_all = finishing(s, "all")
            block = s.enter_context(nc.Block())

            def finish(engine, late_part, all_parts):
                broken_edges = engine.value_load(flag[0:1, 0:1], min_val=0, max_val=1)
                with engine.If(broken_edges == 0):
                    late_part(engine, late_chunks)
                with engine.Else():
                    all_parts(engine, range(CHUNKS))

            @block.tensor
            def _(pe):
                finish(pe, turn_late, turn_all)

            @block.vector
            def _(dve):
                finish(dve, add_late, add_all)

            @block.sync
            def _(sp):
                finish(sp, store_late, store_all)


def node_major(a):
    pad = np.zeros((NODES_PAD - NODES, FEAT), a.dtype)
    rows = np.concatenate([a, pad]).reshape(BLOCKS, P, FEAT)
    return np.ascontiguousarray(rows.transpose(1, 0, 2)).reshape(P, BLOCKS * FEAT)


def edge_major(a, pad):
    a = np.concatenate([a.reshape(-1), np.full(EDGES_PAD - EDGES, pad, a.dtype)])
    return np.ascontiguousarray(a.reshape(TILES, P).T)


def kernel(x, src, dst, edge_attr_32, edge_type_32, edge_weight1, L0_gnn_W1, L0_gnn_b1, L0_gnn_W2, L0_gnn_b2,
           L0_gnn_Wn, L0_gnn_bn, L1_gnn_W, L1_gnn_loop_weight, L1_gnn_h_bias):
    import concourse.bacc as bacc
    from concourse.bass_utils import run_bass_kernel_spmd

    (x, src, dst, edge_attr, edge_type, weight, w1, b1, w2, b2, wn, bn, w_rel, w_loop, bias) = (
        np.asarray(a) for a in (x, src, dst, edge_attr_32, edge_type_32, edge_weight1, L0_gnn_W1, L0_gnn_b1, L0_gnn_W2,
                                L0_gnn_b2, L0_gnn_Wn, L0_gnn_bn, L1_gnn_W, L1_gnn_loop_weight, L1_gnn_h_bias))
    f = np.float32
    dst_flat = np.concatenate([dst, np.full(EDGES_PAD - EDGES, NODES, dst.dtype)])
    w_rel = np.ascontiguousarray(w_rel.transpose(1, 0, 2)).reshape(FEAT, PROJ)
    due = np.maximum(P * (np.arange(MACROS) // 2 - LAG + 1), 0).astype(f)
    arrays = {
        "x_in": node_major(x),
        "src_in": edge_major(src, 0),
        "type_in": edge_major(edge_type, 0),
        "norm_in": edge_major(weight, 0),
        "dst_in": edge_major(dst, NODES),
        "dst_row": dst_flat[None, :],
        "dst_first": np.ascontiguousarray(dst_flat[::MACRO])[None, :],
        "due_in": due[None, :],
        "edges_t": np.ascontiguousarray(np.concatenate([edge_attr, np.zeros((EDGES_PAD - EDGES, EDGE_F), f)]).T),
        "w_pre_in": np.concatenate([w1[0:FEAT], w1[FEAT:2 * FEAT], wn], axis=1),
        "bias_pre_in": np.concatenate([np.zeros(HID, f), b1] + [bn] * GROUP_BLOCKS)[None, :],
        "w_edge_in": np.ascontiguousarray(w1[2 * FEAT:]),
        "w2_in": np.concatenate([w2, np.zeros((HID, 1), f)], axis=1),
        "b2_in": np.concatenate([b2, np.ones(1, f)])[None, :],
        "w_proj_in": np.concatenate([w_rel, w_loop], axis=1),
        "bias_in": bias[None, :],
        "ident_in": np.eye(P, dtype=f),
        "window_row": np.arange(WINDOW, dtype=f)[None, :],
        "window_col": np.arange(P, dtype=f)[:, None],
    }
    nc = bacc.Bacc("TRN2", target_bir_lowering=False, num_devices=1)
    args = [nc.dram_tensor(n, a.shape, mybir.dt.from_np(a.dtype), kind="ExternalInput").ap() for n, a in arrays.items()]
    out = nc.dram_tensor("out", (P, BLOCKS * FEAT), mybir.dt.float32, kind="ExternalOutput").ap()
    gnn_kernel(nc, *args, out)
    got = run_bass_kernel_spmd(nc, [arrays], core_ids=[0]).results[0]["out"]
    return np.ascontiguousarray(np.asarray(got).reshape(P, BLOCKS, FEAT).transpose(1, 0, 2)).reshape(NODES_PAD, FEAT)[:NODES]
```
